# Optimizing a Trainium2 kernel written in Bass

```python
import numpy as np
import jax
import jax.numpy as jnp

def _softmax(x, axis=-1):
    return jax.nn.softmax(x, axis=axis)

def _gelu(x):
    return jax.nn.gelu(x, approximate=True)

def _silu(x):
    return jax.nn.silu(x)

def _sigmoid(x):
    return jax.nn.sigmoid(x)

def _layernorm(x, axis=-1, eps=1e-05):
    m = jnp.mean(x, axis=axis, keepdims=True)
    v = jnp.var(x, axis=axis, keepdims=True)
    return (x - m) / jnp.sqrt(v + eps)

def _scatter_add(tgt, idx, src, axis=0):
    return tgt.at[idx].add(src)

def _segment_sum(src, seg, n):
    return jax.ops.segment_sum(src, seg, n)
kernel_name = 'mk_vit_tower_d1_tok_img1024_r4_1e751f'

def setup_inputs(seed: int=0):
    np.random.seed(seed)
    _w = jnp.asarray

    def _rec_inputs():
        import jax
        import jax.numpy as jnp
        _rk = jax.random.key(seed)
        x = -7.10856e-05 + 0.999911 * jax.random.normal(jax.random.fold_in(_rk, 1), (2, 1, 1024, 256), jnp.float32)
        return x
    x = _rec_inputs()

    def _L0_tok_setup():
        import jax, jax.numpy as jnp
        import numpy as np
        B, T, X, D, H = (16, 1, 1024, 256, 128)
        key = jax.random.key(seed)
        k0, k1, k2 = jax.random.split(key, 3)
        s1 = 1.0 / np.sqrt(D)
        s2 = 1.0 / np.sqrt(H)
        return {'encoder_outputs': jax.random.normal(k0, (B, T, X, D), dtype=jnp.float32), 'W1': jax.random.uniform(k1, (D, H), minval=-s1, maxval=s1, dtype=jnp.float32), 'b1': jnp.zeros((H,), dtype=jnp.float32), 'W2': jax.random.uniform(k2, (H, 1), minval=-s2, maxval=s2, dtype=jnp.float32), 'b2': jnp.zeros((1,), dtype=jnp.float32)}
    _L0_tok_all = _L0_tok_setup()
    _L0_tok_in = {k: v for k, v in _L0_tok_all.items() if k in ('W1', 'b1', 'W2', 'b2')}
    del _L0_tok_all

    def _L0_attn_setup():
        import jax, jax.numpy as jnp
        import numpy as np
        N_EMBD = 256
        N_HEAD = 16
        HEAD_DIM = N_EMBD // N_HEAD
        KV_RANK = 64
        Q_RANK = 128
        ROPE_DIM = 32
        B, T = (2, 512)
        EPS = 1e-06

        def _rope_tables(T, dim):
            inv_freq = 1.0 / 10000.0 ** (np.arange(0, dim, 2, dtype=np.float32) / dim)
            t = np.arange(T, dtype=np.float32)
            freqs = np.outer(t, inv_freq)
            emb = np.concatenate([freqs, freqs], -1)
            return (jnp.asarray(np.cos(emb)), jnp.asarray(np.sin(emb)))

        def _apply_rope(x, cos, sin):
            d2 = x.shape[-1] // 2
            x1, x2 = (x[..., :d2], x[..., d2:])
            rot = jnp.concatenate([-x2, x1], axis=-1)
            return x * cos[None, None, :, :] + rot * sin[None, None, :, :]
        key = jax.random.key(seed)
        ks = jax.random.split(key, 10)

        def w(k, fan_in, fan_out):
            return jax.random.normal(k, (fan_in, fan_out), dtype=jnp.float32) * fan_in ** (-0.5)
        return {'x': jax.random.normal(ks[0], (B, T, N_EMBD), dtype=jnp.float32), 'W_kv': w(ks[1], N_EMBD, KV_RANK), 'g_kv': jnp.ones((KV_RANK,), dtype=jnp.float32), 'W_kdec': w(ks[2], KV_RANK, N_HEAD * HEAD_DIM), 'W_vdec': w(ks[3], KV_RANK, N_HEAD * HEAD_DIM), 'W_q': w(ks[4], N_EMBD, Q_RANK), 'W_qdec': w(ks[5], Q_RANK, N_HEAD * HEAD_DIM), 'W_krope': w(ks[6], N_EMBD, N_HEAD * ROPE_DIM), 'W_qrope': w(ks[7], Q_RANK, N_HEAD * ROPE_DIM), 'W_o': w(ks[8], N_HEAD * HEAD_DIM, N_EMBD)}
    _L0_attn_all = _L0_attn_setup()
    _L0_attn_in = {k: v for k, v in _L0_attn_all.items() if k in ('W_kv', 'g_kv', 'W_kdec', 'W_vdec', 'W_q', 'W_qdec', 'W_krope', 'W_qrope', 'W_o')}
    del _L0_attn_all

    def _L0_ffn_setup():
        import jax, jax.numpy as jnp
        import numpy as np
        E = 8
        K = 2
        S = 1
        THRESHOLD = 0.7
        NORM_TOPK = True
        H = 256
        F = 256
        B, SEQ = (2, 256)
        key = jax.random.key(seed)
        k1, k2, k3, k4, k5 = jax.random.split(key, 5)
        hidden_states = jax.random.normal(k1, (B, SEQ, H), jnp.float32)
        gate_weight = jax.random.normal(k2, (E, H), jnp.float32) * 0.02
        gate_up_proj = jax.random.normal(k3, (E, 2 * F, H), jnp.float32) * 0.02
        down_proj = jax.random.normal(k4, (E, H, F), jnp.float32) * 0.02
        sim = jax.random.uniform(k5, (E, E), jnp.float32)
        sim = (sim + sim.T) / 2.0
        sim = sim.at[jnp.arange(E), jnp.arange(E)].set(1.0)
        return {'hidden_states': hidden_states, 'gate_weight': gate_weight, 'gate_up_proj': gate_up_proj, 'down_proj': down_proj, 'similarity_matrix': sim}
    _L0_ffn_all = _L0_ffn_setup()
    _L0_ffn_in = {k: v for k, v in _L0_ffn_all.items() if k in ('gate_weight', 'gate_up_proj', 'down_proj', 'similarity_matrix')}
    del _L0_ffn_all
    return {'x': x, 'L0_tok_W1': _L0_tok_in['W1'], 'L0_tok_b1': _L0_tok_in['b1'], 'L0_tok_W2': _L0_tok_in['W2'], 'L0_tok_b2': _L0_tok_in['b2'], 'L0_attn_W_kv': _L0_attn_in['W_kv'], 'L0_attn_g_kv': _L0_attn_in['g_kv'], 'L0_attn_W_kdec': _L0_attn_in['W_kdec'], 'L0_attn_W_vdec': _L0_attn_in['W_vdec'], 'L0_attn_W_q': _L0_attn_in['W_q'], 'L0_attn_W_qdec': _L0_attn_in['W_qdec'], 'L0_attn_W_krope': _L0_attn_in['W_krope'], 'L0_attn_W_qrope': _L0_attn_in['W_qrope'], 'L0_attn_W_o': _L0_attn_in['W_o'], 'L0_ffn_gate_weight': _L0_ffn_in['gate_weight'], 'L0_ffn_gate_up_proj': _L0_ffn_in['gate_up_proj'], 'L0_ffn_down_proj': _L0_ffn_in['down_proj'], 'L0_ffn_similarity_matrix': _L0_ffn_in['similarity_matrix']}

def reference(x, L0_tok_W1, L0_tok_b1, L0_tok_W2, L0_tok_b2, L0_attn_W_kv, L0_attn_g_kv, L0_attn_W_kdec, L0_attn_W_vdec, L0_attn_W_q, L0_attn_W_qdec, L0_attn_W_krope, L0_attn_W_qrope, L0_attn_W_o, L0_ffn_gate_weight, L0_ffn_gate_up_proj, L0_ffn_down_proj, L0_ffn_similarity_matrix):
    import jax
    import jax.numpy as jnp

    def _L0_tok_ref(encoder_outputs, W1, b1, W2, b2):
        import jax, jax.numpy as jnp
        import numpy as np
        B, T, X, D, H = (16, 1, 1024, 256, 128)
        h = jnp.tanh(encoder_outputs @ W1 + b1)
        energy = h @ W2 + b2
        energy = jnp.transpose(energy, (0, 3, 2, 1))
        weights = jax.nn.softmax(jnp.squeeze(energy, -1), axis=1)
        out = (encoder_outputs * weights[..., None]).sum(axis=1)
        return out

    def _L0_attn_ref(x, W_kv, g_kv, W_kdec, W_vdec, W_q, W_qdec, W_krope, W_qrope, W_o):
        import jax, jax.numpy as jnp
        import numpy as np
        N_EMBD = 256
        N_HEAD = 16
        HEAD_DIM = N_EMBD // N_HEAD
        KV_RANK = 64
        Q_RANK = 128
        ROPE_DIM = 32
        B, T = (2, 512)
        EPS = 1e-06

        def _rope_tables(T, dim):
            inv_freq = 1.0 / 10000.0 ** (np.arange(0, dim, 2, dtype=np.float32) / dim)
            t = np.arange(T, dtype=np.float32)
            freqs = np.outer(t, inv_freq)
            emb = np.concatenate([freqs, freqs], -1)
            return (jnp.asarray(np.cos(emb)), jnp.asarray(np.sin(emb)))

        def _apply_rope(x, cos, sin):
            d2 = x.shape[-1] // 2
            x1, x2 = (x[..., :d2], x[..., d2:])
            rot = jnp.concatenate([-x2, x1], axis=-1)
            return x * cos[None, None, :, :] + rot * sin[None, None, :, :]
        Bx, Tx, C = x.shape
        kv_c = x @ W_kv
        kv_c = kv_c * jax.lax.rsqrt(jnp.mean(kv_c * kv_c, axis=-1, keepdims=True) + EPS) * g_kv
        q_c = x @ W_q

        def heads(y, d):
            return y.reshape(Bx, Tx, N_HEAD, d).transpose(0, 2, 1, 3)
        k_content = heads(kv_c @ W_kdec, HEAD_DIM)
        v = heads(kv_c @ W_vdec, HEAD_DIM)
        q_content = heads(q_c @ W_qdec, HEAD_DIM)
        k_rope = heads(x @ W_krope, ROPE_DIM)
        q_rope = heads(q_c @ W_qrope, ROPE_DIM)
        cos, sin = _rope_tables(Tx, ROPE_DIM)
        q_rope = _apply_rope(q_rope, cos, sin)
        k_rope = _apply_rope(k_rope, cos, sin)
        q = jnp.concatenate([q_content, q_rope], axis=-1)
        k = jnp.concatenate([k_content, k_rope], axis=-1)
        scale = 1.0 / jnp.sqrt(jnp.float32(q.shape[-1]))
        scores = jnp.einsum('bhqd,bhkd->bhqk', q, k) * scale
        causal = jnp.tril(jnp.ones((Tx, Tx), dtype=bool))
        scores = jnp.where(causal[None, None], scores, jnp.float32(-jnp.inf))
        attn = jax.nn.softmax(scores, axis=-1)
        out = jnp.einsum('bhqk,bhkd->bhqd', attn, v)
        out = out.transpose(0, 2, 1, 3).reshape(Bx, Tx, N_HEAD * HEAD_DIM)
        return out @ W_o

    def _L0_ffn_ref(hidden_states, gate_weight, gate_up_proj, down_proj, similarity_matrix):
        import jax, jax.numpy as jnp
        import numpy as np
        E = 8
        K = 2
        S = 1
        THRESHOLD = 0.7
        NORM_TOPK = True
        H = 256
        F = 256
        B, SEQ = (2, 256)
        b, s, h = hidden_states.shape
        x = hidden_states.reshape(-1, h)
        N = x.shape[0]
        logits = x @ gate_weight.T
        probs = jax.nn.softmax(logits.astype(jnp.float32), axis=-1)
        top_w, top_i = jax.lax.top_k(probs, K)
        if NORM_TOPK:
            top_w = top_w / jnp.clip(jnp.sum(top_w, -1, keepdims=True), 1e-12)
        primary_mask = jnp.zeros((E,), bool).at[top_i[:, :S].reshape(-1)].set(True)
        sim = jnp.where(primary_mask[None, :], similarity_matrix.astype(jnp.float32), -jnp.inf)
        best_j = jnp.argmax(sim, axis=-1)
        best_sim = jnp.max(sim, axis=-1)
        ids = jnp.arange(E)
        expert_map = jnp.where(~primary_mask & (best_sim >= THRESHOLD), best_j, ids)
        rerouted = expert_map[top_i]
        rows = jnp.arange(N)[:, None]
        dense = jnp.zeros((N, E), top_w.dtype).at[rows, rerouted].add(top_w)
        fw, fi = jax.lax.top_k(dense, K)
        combine = jnp.zeros((N, E), fw.dtype).at[rows, fi].add(jnp.where(fw > 0, fw, 0.0))
        gu = jnp.einsum('nh,efh->enf', x, gate_up_proj)
        g, u = jnp.split(gu, 2, axis=-1)
        hmid = jax.nn.silu(g) * u
        y = jnp.einsum('enf,ehf->enh', hmid, down_proj)
        out = jnp.einsum('ne,enh->nh', combine, y)
        return out.reshape(b, s, h)
    h = _L0_tok_ref(x, L0_tok_W1, L0_tok_b1, L0_tok_W2, L0_tok_b2)
    h = h + _L0_attn_ref(_layernorm(h, axis=-1), L0_attn_W_kv, L0_attn_g_kv, L0_attn_W_kdec, L0_attn_W_vdec, L0_attn_W_q, L0_attn_W_qdec, L0_attn_W_krope, L0_attn_W_qrope, L0_attn_W_o)
    h = h + _L0_ffn_ref(_layernorm(h, axis=-1), L0_ffn_gate_weight, L0_ffn_gate_up_proj, L0_ffn_down_proj, L0_ffn_similarity_matrix)
    return h

_drawn_inputs = setup_inputs


def setup_inputs(seed=0):
    import zlib

    import numpy as np

    out = dict(_drawn_inputs(seed))
    spreads = {'L0_tok_b1': (0.0, 0.1), 'L0_attn_g_kv': (1.0, 0.2)}
    factors = {'L0_ffn_gate_weight': 5.452, 'L0_ffn_gate_up_proj': 4.741, 'L0_ffn_down_proj': 4.734}
    for name, (base, spread) in spreads.items():
        noise = np.random.default_rng([zlib.crc32(name.encode()), seed]).standard_normal(out[name].shape)
        drawn = base * np.exp(spread * noise) if base else spread * noise
        out[name] = jnp.asarray(drawn.astype(out[name].dtype))
    for name, factor in factors.items():
        out[name] = (out[name] * factor).astype(out[name].dtype)
    return out
```

```python
from contextlib import ExitStack

import concourse.bass as bass
from concourse import mybir

F32 = mybir.dt.float32
F32R = mybir.dt.float32r
ALU = mybir.AluOpType
ACT = mybir.ActivationFunctionType
AX = mybir.AxisListType

P = 128
B, T, D = 2, 1024, 256
TT = B * T // P
BT = T // P
DC = D // P
HEADS, CON, ROPE = 16, 16, 32
HD = CON + ROPE
J = 4
G = HEADS // J
KVR, QR = 64, 128
E, F = 8, 256
FC = F // P
TOKH = 128
W = 512
NW = B * T // W
BIG = float(2 ** 100)
LOWEST = -3.0e38


class Chain:

    def __init__(self, eng, sem, base=0):
        self.eng, self.sem, self.base, self.n = eng, sem, base, 0

    def did(self, ins):
        self.n += 1
        ins.then_inc(self.sem, 1)
        return ins

    def settle(self):
        self.eng.wait_ge(self.sem, self.base + self.n)


def head_start(eng, *sems):
    for s in sems:
        eng.sem_inc(s, 1)


def three(pe, out, stat, mov, first=True, last=True):
    (sh, sl), (mh, ml) = stat, mov
    pe.matmul(out, sh, mh, start=first, stop=False)
    pe.matmul(out, sh, ml, start=False, stop=False)
    return pe.matmul(out, sl, mh, start=False, stop=last)


def prepare(nc, d, k):
    with ExitStack() as ctx:
        def sb(name, shape, dt=F32):
            return ctx.enter_context(nc.sbuf_tensor(name, shape, dt))

        def sem(name):
            return ctx.enter_context(nc.semaphore(name))

        xT = sb("xT", [P, DC, B * T])
        xin = sb("xin", [P, TT, D])
        w1 = sb("w1", [P, DC, TOKH])
        w2 = sb("w2", [P, 1])
        b1 = sb("b1", [P, 1])
        b2 = sb("b2", [P, 1])
        hid = sb("hid", [P, 2, W])
        en = sb("en", [P, TT])
        de = sb("de", [P, TT])
        ex = sb("ex", [P, TT])
        rs = sb("rs", [P, TT])
        wt = sb("wt", [P, TT])
        stats = sb("stats", [P, TT, 6])
        mv = sb("mv", [P, TT, 2])
        ve = sb("ve", [P, TT])
        sd = sb("sd", [P, TT])
        rstd = sb("rstd", [P, TT])
        xn = xin
        wq = sb("wq", [P, DC, QR])
        wqh = sb("wqh", [P, DC, QR], F32R)
        wql = sb("wql", [P, DC, QR], F32R)
        wkv = sb("wkv", [P, DC, KVR])
        wkvh = sb("wkvh", [P, DC, KVR], F32R)
        wkvl = sb("wkvl", [P, DC, KVR], F32R)
        gkv = sb("gkv", [P, KVR])
        kvsq = sb("kvsq", [P, TT, KVR])
        kvn = sb("kvn", [P, TT, KVR])
        kvd = sb("kvd", [P, TT, 2 * KVR])
        kvm = sb("kvm", [P, TT])
        kvs = sb("kvs", [P, TT])
        kvr = sb("kvr", [P, TT])
        kvhi = sb("kvhi", [P, 2, W], F32R)
        wkr = sb("wkr", [P, DC, HEADS * ROPE])
        wqx = sb("wqx", [P, G, J * HD])
        wkx = sb("wkx", [P, G, 2 * J * CON])
        lowrow = sb("lowrow", [P, 1])
        mask1 = sb("mask1", [P, P])
        mask2 = sb("mask2", [P, P])

        ps = [ctx.enter_context(nc.psum_tensor(f"pa{i}", [P, W], F32)) for i in range(8)]

        xT_in, x_in, tok_w_in, low_w_in, dec_w_in, tab_in = (sem(n) for n in (
            "xT_in",
            "x_in", "tok_w_in", "low_w_in", "dec_w_in", "tab_in"))
        hid_ps, hid_ready, en_ps = sem("hid_ps"), sem("hid_ready"), sem("en_ps")
        diff_ready, exp_ready, var_ready, sd_ready = (sem(n) for n in ("diff_ready", "exp_ready", "var_ready", "sd_ready"))
        xn_ready, turned, hi_ready, lo_ready = (sem(n) for n in ("xn_ready", "turned", "hi_ready", "lo_ready"))
        low_split, const_ready, kv_ps, kv_sq, kv_mean, kv_sd = (sem(n) for n in (
            "low_split", "const_ready", "kv_ps", "kv_sq", "kv_mean", "kv_sd"))
        qc_ps, qc_hi, qc_lo = sem("qc_ps"), sem("qc_hi"), sem("qc_lo")
        kvn_ready, kv_turned, kv_hi, kv_split = sem("kvn_ready"), sem("kv_turned"), sem("kv_hi"), sem("kv_split")
        dve_step, pool_step, mask_in = sem("dve_step"), sem("pool_step"), sem("mask_in")

        with nc.Block() as block:
            @block.sync
            def _(sp):
                for c in range(DC):
                    sp.dma_start(xT[:, c, :], d["xT"][c * P:(c + 1) * P, :]).then_inc(xT_in, 16)
                sp.dma_start(w1[:], d["W1"].rearrange("(c p) h -> p c h", p=P)).then_inc(tok_w_in, 16)
                sp.dma_start(b1[:], d["b1"].rearrange("(p a) -> p a", a=1)).then_inc(tok_w_in, 16)
                sp.dma_start(w2[:], d["W2"]).then_inc(tok_w_in, 16)
                sp.dma_start(b2[:], d["b2"].rearrange("(p a) -> p a", a=1).to_broadcast([P, 1])).then_inc(tok_w_in, 16)
                sp.dma_start(xin[:], d["x"].rearrange("(t p) e -> p t e", p=P)).then_inc(x_in, 16)
                sp.dma_start(wq[:], d["W_q"].rearrange("(c p) r -> p c r", p=P)).then_inc(low_w_in, 16)
                sp.dma_start(wkv[:], d["W_kv"].rearrange("(c p) r -> p c r", p=P)).then_inc(low_w_in, 16)
                sp.dma_start(gkv[:], d["g_kv"].rearrange("(a r) -> a r", a=1).to_broadcast([P, KVR])).then_inc(low_w_in, 16)
                sp.dma_start(wkr[:], d["W_krope"].rearrange("(c p) n -> p c n", p=P)).then_inc(dec_w_in, 16)
                sp.dma_start(wqx[:, :, 0:J * ROPE], d["W_qrope"].rearrange("p (g n) -> p g n", g=G)).then_inc(dec_w_in, 16)
                sp.dma_start(wqx[:, :, J * ROPE:J * HD], d["W_qdec"].rearrange("p (g n) -> p g n", g=G)).then_inc(dec_w_in, 16)
                for r in range(2):
                    rows = slice(r * KVR, (r + 1) * KVR)
                    sp.dma_start(wkx[rows, :, 0:J * CON], d["W_kdec"].rearrange("p (g n) -> p g n", g=G)).then_inc(dec_w_in, 16)
                    sp.dma_start(wkx[rows, :, J * CON:], d["W_vdec"].rearrange("p (g n) -> p g n", g=G)).then_inc(dec_w_in, 16)
                sp.dma_start(k["cos"][:], d["cos"].rearrange("(t p) r -> p t r", p=P)).then_inc(tab_in, 16)
                sp.dma_start(k["sin"][:], d["sin"].rearrange("(t p) r -> p t r", p=P)).then_inc(tab_in, 16)
                sp.wait_ge(tab_in, 32)

            @block.gpsimd
            def _(pool):
                step = Chain(pool, pool_step)
                step.did(pool.memset(k["ident"][:], 0.0))
                step.did(pool.memset(mask1[:], 0.0))
                step.did(pool.memset(mask2[:], 0.0))
                step.did(pool.memset(lowrow[:], -1.0))
                step.settle()
                step.did(pool.affine_select(out=k["ident"][:], in_=k["ident"][:], compare_op=ALU.not_equal, fill=1.0,
                                            base=0, pattern=[[-1, P]], channel_multiplier=1))
                step.did(pool.affine_select(out=mask1[:], in_=mask1[:], compare_op=ALU.is_ge, fill=-BIG,
                                            base=0, pattern=[[-1, P]], channel_multiplier=1))
                step.did(pool.affine_select(out=mask2[:], in_=mask2[:], compare_op=ALU.is_ge, fill=-BIG,
                                            base=0, pattern=[[1, P]], channel_multiplier=-1))
                step.did(pool.memset(lowrow[0:KVR, :], 0.0))
                step.settle()
                pool.tensor_copy(k["ident_r"][:], k["ident"][:])
                pool.tensor_copy(k["mask_qk"][:], mask1[:])
                pool.tensor_copy(k["mask_kq"][:], mask2[:]).then_inc(const_ready, 1)
                pool.wait_ge(low_w_in, 48)
                step.did(pool.tensor_copy(wqh[:], wq[:]))
                step.did(pool.tensor_copy(wkvh[:], wkv[:]))
                step.settle()
                pool.tensor_tensor(wql[:], wq[:], wqh[:].bitcast(F32), ALU.subtract)
                pool.tensor_tensor(wkvl[:], wkv[:], wkvh[:].bitcast(F32), ALU.subtract).then_inc(low_split, 1)
                pool.wait_ge(dec_w_in, 16 * 7)
                for raw, name in ((wkr, "wkr"), (wqx, "wqx"), (wkx, "wkx")):
                    step.did(pool.tensor_copy(k[name + "h"][:], raw[:]))
                step.settle()
                for raw, name in ((wkr, "wkr"), (wqx, "wqx"), (wkx, "wkx")):
                    pool.tensor_tensor(k[name + "l"][:], raw[:], k[name + "h"][:].bitcast(F32), ALU.subtract)
                step.did(pool.memset(k["vst"][:], 0.0))
                step.settle()
                step.did(pool.memset(k["vst"][:, :, :, CON:CON + 1], 1.0))
                step.settle()

            def energies(pe, n):
                pe.wait_ge(hid_ready, n + 1)
                for i in range(4):
                    t = 4 * n + i
                    last = pe.matmul(ps[2][:, t:t + 1], hid[:, n % 2, i * P:(i + 1) * P], w2[:], start=True, stop=True)
                last.then_inc(en_ps, 1)

            @block.tensor
            def _(pe):
                pe.wait_ge(xT_in, 32)
                pe.wait_ge(tok_w_in, 64)
                for n in range(NW):
                    if n >= 2:
                        pe.wait_ge(hid_ready, n - 1)
                    for c in range(DC):
                        last = pe.matmul(ps[n % 2][:], w1[:, c, :], xT[:, c, n * W:(n + 1) * W],
                                         start=(c == 0), stop=(c == DC - 1))
                    last.then_inc(hid_ps, 1)
                    if n >= 1:
                        energies(pe, n - 1)
                energies(pe, NW - 1)
                pe.wait_ge(const_ready, 1)
                for n in range(NW):
                    pe.wait_ge(xn_ready, 4 * n + 4)
                    for c in range(DC):
                        m = n * DC + c
                        if m >= 4:
                            pe.wait_ge(lo_ready, m - 3)
                        for i in range(4):
                            last = pe.transpose(ps[4 + m % 4][:, i * P:(i + 1) * P],
                                                xn[:, 4 * n + i, c * P:(c + 1) * P], k["ident"][:])
                        last.then_inc(turned, 1)
                pe.wait_ge(low_split, 1)
                for n in range(NW):
                    pe.wait_ge(lo_ready, DC * n + 2)
                    cols = slice(n * W, (n + 1) * W)
                    for t in range(4 * n, 4 * n + 4):
                        tok = slice(t * P, (t + 1) * P)
                        out = ps[2 + t // 8][:, (t % 8) * KVR:(t % 8 + 1) * KVR]
                        if t == 0:
                            pe.wait_ge(diff_ready, 1)
                        for c in range(DC):
                            last = three(pe, out, (k["xh"][:, c, tok], k["xl"][:, c, tok]),
                                         (wkvh[:, c, :], wkvl[:, c, :]), c == 0, c == DC - 1)
                    last.then_inc(kv_ps, 1)
                    if n >= 2:
                        pe.wait_ge(qc_lo, n - 1)
                    for c in range(DC):
                        last = three(pe, ps[n % 2][:], (wqh[:, c, :], wql[:, c, :]),
                                     (k["xh"][:, c, cols], k["xl"][:, c, cols]), c == 0, c == DC - 1)
                    last.then_inc(qc_ps, 1)
                pe.wait_ge(kvn_ready, 1)
                for n in range(NW):
                    for i in range(4):
                        last = pe.transpose(ps[4 + n][:, i * P:(i + 1) * P], kvd[:, 4 * n + i], k["ident"][:])
                    last.then_inc(kv_turned, 1)

            @block.scalar
            def _(act):
                act.wait_ge(tok_w_in, 64)
                for n in range(NW):
                    act.wait_ge(hid_ps, n + 1)
                    if n >= 2:
                        act.wait_ge(en_ps, n - 1)
                    act.activation(hid[:, n % 2, :], ps[n % 2][:], ACT.Tanh, bias=b1[:, 0:1]).then_inc(hid_ready, 1)
                act.wait_ge(diff_ready, 1)
                act.activation(ex[:], de[:], ACT.Exp).then_inc(exp_ready, 1)
                act.wait_ge(var_ready, 1)
                act.activation(sd[:], ve[:], ACT.Sqrt).then_inc(sd_ready, 1)
                for n in range(NW):
                    for c in range(DC):
                        m = n * DC + c
                        act.wait_ge(turned, m + 1)
                        act.activation(k["xh"][:, c, n * W:(n + 1) * W], ps[4 + m % 4][:], ACT.Copy).then_inc(hi_ready, 1)
                for n in range(NW):
                    act.wait_ge(qc_ps, n + 1)
                    act.activation(k["qh"][:, n * W:(n + 1) * W], ps[n % 2][:], ACT.Copy).then_inc(qc_hi, 1)
                for r in range(2):
                    act.wait_ge(kv_ps, 2 * r + 2)
                    act.activation(kvsq[:, 8 * r:8 * r + 8, :].rearrange("p t r -> p (t r)"), ps[2 + r][:],
                                   ACT.Square).then_inc(kv_sq, 1)
                act.wait_ge(kv_mean, 1)
                act.activation(kvs[:], kvm[:], ACT.Sqrt).then_inc(kv_sd, 1)
                for n in range(NW):
                    act.wait_ge(kv_turned, n + 1)
                    if n >= 2:
                        act.wait_ge(kv_split, n - 1)
                    act.activation(kvhi[:, n % 2, :], ps[4 + n][:], ACT.Copy).then_inc(kv_hi, 1)

            @block.vector
            def _(dve):
                step = Chain(dve, dve_step)
                dve.memset(k["ones_rows"].bitcast(F32), 1.0)
                dve.memset(k["pmax"][:], LOWEST)
                dve.wait_ge(tok_w_in, 64)
                dve.wait_ge(en_ps, NW)
                step.did(dve.tensor_scalar(en[:], ps[2][:, 0:TT], b2[:, 0:1], None, ALU.add))
                step.settle()
                dve.tensor_tensor(de[:], en[:], en[:], ALU.subtract).then_inc(diff_ready, 1)
                dve.wait_ge(exp_ready, 1)
                step.did(dve.reciprocal(rs[:], ex[:]))
                step.settle()
                step.did(dve.tensor_tensor(wt[:], ex[:], rs[:], ALU.mult))
                dve.wait_ge(x_in, 16)
                step.settle()
                for t in range(TT):
                    step.did(dve.tensor_scalar(k["h"][:, t, :], xin[:, t, :], wt[:, t:t + 1], None, ALU.mult))
                step.settle()
                for t in range(TT):
                    step.did(dve.bn_stats(stats[:, t, :], k["h"][:, t, :]))
                step.settle()
                for t in range(TT):
                    step.did(dve.bn_aggr(mv[:, t, :], stats[:, t, :]))
                step.settle()
                dve.tensor_scalar(ve[:], mv[:, :, 1], 1e-5, None, ALU.add).then_inc(var_ready, 1)
                dve.wait_ge(sd_ready, 1)
                step.did(dve.reciprocal(rstd[:], sd[:]))
                step.settle()
                for t in range(TT):
                    dve.tensor_scalar(xn[:, t, :], k["h"][:, t, :], mv[:, t, 0:1], rstd[:, t:t + 1],
                                      ALU.subtract, ALU.mult).then_inc(xn_ready, 1)
                for n in range(NW):
                    for c in range(DC):
                        m = n * DC + c
                        dve.wait_ge(hi_ready, m + 1)
                        dve.tensor_tensor(k["xl"][:, c, n * W:(n + 1) * W], ps[4 + m % 4][:],
                                          k["xh"][:, c, n * W:(n + 1) * W].bitcast(F32), ALU.subtract).then_inc(lo_ready, 1)
                for n in range(NW):
                    dve.wait_ge(qc_hi, n + 1)
                    dve.tensor_tensor(k["ql"][:, n * W:(n + 1) * W], ps[n % 2][:],
                                      k["qh"][:, n * W:(n + 1) * W].bitcast(F32), ALU.subtract).then_inc(qc_lo, 1)
                dve.wait_ge(kv_sq, 2)
                step.did(dve.tensor_reduce(kvr[:], kvsq[:], AX.X, ALU.add))
                step.settle()
                dve.tensor_scalar(kvm[:], kvr[:], 1.0 / KVR, 1e-6, ALU.mult, ALU.add).then_inc(kv_mean, 1)
                dve.wait_ge(kv_sd, 1)
                step.did(dve.reciprocal(kvr[:], kvs[:]))
                step.settle()
                for r in range(2):
                    step.did(dve.tensor_tensor(
                        kvn[:, 8 * r:8 * r + 8, :], ps[2 + r][:].rearrange("p (t r) -> p t r", r=KVR),
                        kvr[:, 8 * r:8 * r + 8].rearrange("p (t a) -> p t a", a=1).to_broadcast([P, 8, KVR]), ALU.mult))
                step.settle()
                for r in range(2):
                    last = dve.tensor_tensor(kvd[:, :, r * KVR:(r + 1) * KVR], kvn[:],
                                             gkv[:].rearrange("p (a r) -> p a r", a=1).to_broadcast([P, TT, KVR]), ALU.mult)
                last.then_inc(kvn_ready, 1)
                dve.wait_ge(const_ready, 1)
                for n in range(NW):
                    dve.wait_ge(kv_hi, n + 1)
                    dve.scalar_tensor_tensor(out=kvtmp(k, n), in0=kvhi[:, n % 2, :].bitcast(F32), scalar=lowrow[:, 0:1],
                                             in1=ps[4 + n][:], op0=ALU.mult, op1=ALU.add).then_inc(kv_split, 1)


def kvtmp(k, n):
    return k["kv"][:, n * W:(n + 1) * W]


def chunks():
    for t in range(BT):
        for ck in range(t // 4 + 1):
            yield t, ck, min(W, (t + 1) * P - ck * W)


def steps():
    for c in range(BT // 4):
        for kt in range(4 * c + 4):
            yield c, kt, max(0, kt - 4 * c) * P


CH = list(chunks())
ST = list(steps())
NCH, NST = J * len(CH), len(ST)
NSU = J * NST


def attention(nc, k):
    with ExitStack() as ctx:
        def sb(name, shape, dt=F32):
            return ctx.enter_context(nc.sbuf_tensor(name, shape, dt))

        def sem(name):
            return ctx.enter_context(nc.semaphore(name))

        SCALE = float(1.0 / (float(HD) ** 0.5))
        raw = sb("raw", [P, 2, 7 * J * CON])
        roc = sb("roc", [P, 2, 2 * J, ROPE])
        ros = sb("ros", [P, 2, 2 * J, ROPE])
        kraw = sb("kraw", [P, 2, J, HD])
        qd = sb("qd", [P, BT, J, 2, HD])
        khl = sb("khl", [P, BT, J, 2, HD], F32R)
        prob = sb("prob", [P, 8, W])
        mx = sb("mx", [P, J, BT])
        mcol = sb("mcol", [P, J, BT, 2], F32R)
        osb = sb("osb", [P, W])
        rcp = sb("rcp", [P, 4, J])
        kst, qa, qb = k["kst"], k["qa"], k["qb"]
        xh, xl, qh, ql, kv, vst, att = (k[n] for n in ("xh", "xl", "qh", "ql", "kv", "vst", "att"))
        ident, ident_r, mask_qk, mask_kq = (k[n] for n in ("ident", "ident_r", "mask_qk", "mask_kq"))

        prep = [ctx.enter_context(nc.psum_tensor(f"prep{i}", [P, W], F32)) for i in range(2)]
        mxp = [ctx.enter_context(nc.psum_tensor(f"mxp{i}", [P, W], F32)) for i in range(2)]
        sc = [ctx.enter_context(nc.psum_tensor(f"sc{i}", [P, W], F32)) for i in range(2)]
        acc = ctx.enter_context(nc.psum_tensor("acc", [P, W], F32))
        otr = ctx.enter_context(nc.psum_tensor("otr", [P, W], F32))

        (proj_done, raw_ready, arr_ready, k_turned, q_turned, kst_ready, qa_ready, qb_ready, max_ps, max_taken,
         mcol_ready, m_turned, mrow_ready, score_ps, exp_done, av_done, scores_done, o_taken, o_turned, att_ready,
         pool_step, dve_step) = (sem(n) for n in (
             "proj_done", "raw_ready", "arr_ready", "k_turned", "q_turned", "kst_ready", "qa_ready", "qb_ready",
             "max_ps", "max_taken", "mcol_ready", "m_turned", "mrow_ready", "score_ps", "exp_done", "av_done",
             "scores_done", "o_taken", "o_turned", "att_ready", "at_pool_step", "at_dve_step"))

        with nc.Block() as block:
            @block.tensor
            def _(pe):
                def project(g, b, half):
                    for t in range(BT):
                        if t == 0:
                            pe.wait_ge(kst_ready, 1 + 8 * half)
                        elif t == 1:
                            pe.wait_ge(qb_ready, 1 + 8 * half)
                        else:
                            pe.wait_ge(raw_ready, BT * half + t - 1)
                        out = prep[t % 2]
                        tok = slice((b * BT + t) * P, (b * BT + t + 1) * P)
                        cols = bass.ds(g * J * ROPE, J * ROPE)
                        for c in range(DC):
                            three(pe, out[:, 0:J * ROPE], (xh[:, c, tok], xl[:, c, tok]),
                                  (k["wkrh"][:, c, cols], k["wkrl"][:, c, cols]), c == 0, c == DC - 1)
                        three(pe, out[:, J * ROPE:J * (ROPE + HD)], (qh[:, tok], ql[:, tok]),
                              (k["wqxh"][:, bass.ds(g, 1), :], k["wqxl"][:, bass.ds(g, 1), :]))
                        o = out[:, J * (ROPE + HD):7 * J * CON]
                        pe.matmul(o, kv[:, tok], k["wkxh"][:, bass.ds(g, 1), :], start=True, stop=False)
                        pe.matmul(o, kv[:, tok], k["wkxl"][:, bass.ds(g, 1), :], start=False, stop=True).then_inc(proj_done, 1)

                def turn(half):
                    pe.wait_ge(raw_ready, BT * half + BT)
                    for m in range(2 * J):
                        j, hh = m // 2, m % 2
                        if j == 0:
                            pe.wait_ge(arr_ready, 1 + BT * half + 4 * hh + 4)
                        if m:
                            pe.wait_ge(kst_ready, 1 + 8 * half + m)
                        for i in range(4):
                            last = pe.transpose(prep[0][0:2 * HD, i * P:(i + 1) * P],
                                                khl[:, 4 * hh + i, j].rearrange("p a r -> p (a r)").bitcast(F32), ident[:])
                        last.then_inc(k_turned, 1)
                        if m:
                            pe.wait_ge(qb_ready, 1 + 8 * half + m)
                        for i in range(4):
                            last = pe.transpose(prep[1][0:2 * HD, i * P:(i + 1) * P],
                                                qd[:, 4 * hh + i, j].rearrange("p a r -> p (a r)"), ident[:])
                        last.then_inc(q_turned, 1)

                def maxima(half):
                    for j in range(J):
                        pe.wait_ge(kst_ready, 1 + 8 * half + 2 * j + 2)
                        pe.wait_ge(qb_ready, 1 + 8 * half + 2 * j + 2)
                        for i, (t, ck, w) in enumerate(CH):
                            x = len(CH) * j + i
                            pe.wait_ge(max_taken, 1 + NCH * half + max(x - 1, 0))
                            out = mxp[x % 2]
                            q = slice(t * P, (t + 1) * P)
                            diagonal = ck == t // 4
                            keys = kst[0:2 * HD, j, ck * W:ck * W + w]
                            pe.matmul(out[:, 0:w], qa[0:2 * HD, j, q], keys, start=True, stop=False)
                            last = pe.matmul(out[:, 0:w], qb[0:2 * HD, j, q], keys, start=False, stop=not diagonal)
                            if diagonal:
                                last = pe.matmul(out[:, w - P:w], ident_r[:], mask_qk[:], start=False, stop=True)
                            last.then_inc(max_ps, 1)

                def turn_maxima(half):
                    pe.wait_ge(mcol_ready, half + 1)
                    for m in range(2 * J):
                        j, hh = m // 2, m % 2
                        pe.wait_ge(mrow_ready, 1 + 8 * half + max(m - 1, 0))
                        for i in range(4):
                            last = pe.transpose(mxp[m % 2][0:2, i * P:(i + 1) * P],
                                                mcol[:, j, 4 * hh + i, :].bitcast(F32), ident[:])
                        last.then_inc(m_turned, 1)

                def score(half, s):
                    c, kt, lo = ST[s]
                    for j in range(J):
                        x = J * s + j
                        if kt == 0:
                            pe.wait_ge(mrow_ready, 1 + 8 * half + 2 * j + c + 1)
                        pe.wait_ge(exp_done, 1 + NSU * half + max(x - 1, 0))
                        q = slice(c * W + lo, (c + 1) * W)
                        key = slice(kt * P, (kt + 1) * P)
                        out = sc[x % 2]
                        diagonal = kt >= 4 * c
                        pe.matmul(out[:, lo:W], kst[:, j, key], qa[:, j, q], start=True, stop=False)
                        last = pe.matmul(out[:, lo:W], kst[0:2 * HD, j, key], qb[0:2 * HD, j, q], start=False, stop=not diagonal)
                        if diagonal:
                            last = pe.matmul(out[:, lo:lo + P], ident_r[:], mask_kq[:], start=False, stop=True)
                        last.then_inc(score_ps, 1)

                def values(half, s):
                    c, kt, lo = ST[s]
                    pe.wait_ge(exp_done, 1 + NSU * half + J * (s + 1))
                    if kt == 0:
                        pe.wait_ge(o_taken, 1 + 2 * half + c)
                    for j in range(J):
                        last = pe.matmul(acc[32 * j:32 * j + 32, lo:W], vst[:, kt, j, :], prob[:, (J * s + j) % 8, lo:W],
                                         start=(kt == 0), stop=(kt == 4 * c + 3))
                    last.then_inc(av_done, 1)

                def turn_outputs(half, c):
                    pe.wait_ge(o_taken, 1 + 2 * half + c + 1)
                    pe.wait_ge(att_ready, 1 + 2 * half + c)
                    for i in range(4):
                        last = pe.transpose(otr[:, i * P:(i + 1) * P], osb[:, i * P:(i + 1) * P], ident[:])
                    last.then_inc(o_turned, 1)

                head_start(pe, k_turned, q_turned, av_done, o_turned)
                with pe.Fori(0, G) as g:
                    for b in range(B):
                        half = g * 2 + b
                        project(g, b, half)
                        turn(half)
                        maxima(half)
                        turn_maxima(half)
                        for s in range(NST):
                            score(half, s)
                            if s:
                                values(half, s - 1)
                            if s == 5:
                                turn_outputs(half, 0)
                        values(half, NST - 1)
                        turn_outputs(half, 1)

            @block.scalar
            def _(act):
                def raws(half):
                    for t in range(BT):
                        act.wait_ge(proj_done, BT * half + t + 1)
                        act.wait_ge(arr_ready, 1 + BT * half + max(t - 1, 0))
                        act.activation(raw[:, t % 2, :], prep[t % 2][:, 0:7 * J * CON], ACT.Copy).then_inc(raw_ready, 1)

                def operands(half):
                    act.wait_ge(av_done, 1 + NST * half)
                    for m in range(2 * J):
                        j, hh = m // 2, m % 2
                        cols = slice(hh * W, (hh + 1) * W)
                        act.wait_ge(k_turned, 1 + 8 * half + m + 1)
                        act.activation(kst[0:2 * HD, j, cols], prep[0][0:2 * HD, :], ACT.Copy).then_inc(kst_ready, 1)
                        act.wait_ge(q_turned, 1 + 8 * half + m + 1)
                        act.activation(qa[0:2 * HD, j, cols], prep[1][0:2 * HD, :], ACT.Copy).then_inc(qa_ready, 1)

                def exps(half):
                    for s, (c, kt, lo) in enumerate(ST):
                        act.wait_ge(av_done, 1 + NST * half + max(s - 1, 0))
                        for j in range(J):
                            x = J * s + j
                            act.wait_ge(score_ps, NSU * half + x + 1)
                            act.activation(prob[:, x % 8, lo:W], sc[x % 2][:, lo:W], ACT.Exp, scale=SCALE).then_inc(exp_done, 1)

                head_start(act, kst_ready, exp_done)
                with act.Fori(0, G) as g:
                    for b in range(B):
                        half = g * 2 + b
                        raws(half)
                        operands(half)
                        exps(half)

            @block.gpsimd
            def _(pool):
                PSTEP = 2 * BT
                head_start(pool, arr_ready)
                with pool.Fori(0, G) as g:
                    for b in range(B):
                        half = g * 2 + b
                        pool.wait_ge(q_turned, 1 + 8 * half)
                        pool.wait_ge(k_turned, 1 + 8 * half)
                        pool.wait_ge(av_done, 1 + NST * half)
                        for t in range(BT):
                            u = t % 2
                            pool.wait_ge(raw_ready, BT * half + t + 1)
                            rope = raw[:, u, 0:2 * J * ROPE].rearrange("p (h r) -> p h r", r=ROPE)
                            cos = k["cos"][:, t:t + 1, :].to_broadcast([P, 2 * J, ROPE])
                            pool.tensor_tensor(roc[:, u], rope, cos, ALU.mult)
                            for lo, hi in ((0, ROPE // 2), (ROPE // 2, 0)):
                                sin = k["sin"][:, t:t + 1, lo:lo + ROPE // 2].to_broadcast([P, 2 * J, ROPE // 2])
                                last = pool.tensor_tensor(ros[:, u, :, lo:lo + ROPE // 2], rope[:, :, hi:hi + ROPE // 2], sin, ALU.mult)
                            q0, k0, v0 = 2 * J * ROPE, 2 * J * ROPE + J * CON, 2 * J * ROPE + 2 * J * CON
                            for r in range(2):
                                pool.tensor_copy(qd[:, t, :, r, 0:CON], raw[:, u, q0:k0].rearrange("p (h r) -> p h r", r=CON))
                            pool.tensor_copy(kraw[:, u, :, 0:CON], raw[:, u, k0:v0].rearrange("p (h r) -> p h r", r=CON))
                            pool.tensor_copy(khl[:, t, :, 0, 0:CON], raw[:, u, k0:v0].rearrange("p (h r) -> p h r", r=CON))
                            pool.tensor_copy(vst[:, t, :, 0:CON], raw[:, u, v0:].rearrange("p (h r) -> p h r", r=CON)).then_inc(pool_step, 1)
                            pool.wait_ge(pool_step, PSTEP * half + 2 * t + 1)
                            for r in range(2):
                                pool.tensor_tensor(qd[:, t, :, r, CON:HD], roc[:, u, J:2 * J], ros[:, u, J:2 * J], ALU.add)
                            pool.tensor_tensor(kraw[:, u, :, CON:HD], roc[:, u, 0:J], ros[:, u, 0:J], ALU.add)
                            pool.tensor_tensor(khl[:, t, :, 0, CON:HD], roc[:, u, 0:J], ros[:, u, 0:J],
                                               ALU.add).then_inc(pool_step, 1)
                            pool.wait_ge(pool_step, PSTEP * half + 2 * t + 2)
                            pool.tensor_tensor(khl[:, t, :, 1, :], kraw[:, u], khl[:, t, :, 0, :].bitcast(F32),
                                               ALU.subtract).then_inc(arr_ready, 1)

            @block.vector
            def _(dve):
                DSTEP = 2 + 2
                head_start(dve, qb_ready, max_taken, mrow_ready, o_taken, att_ready)
                with dve.Fori(0, G) as g:
                    for b in range(B):
                        half = g * 2 + b
                        step = Chain(dve, dve_step, DSTEP * half)
                        for m in range(2 * J):
                            j, hh = m // 2, m % 2
                            cols = slice(hh * W, (hh + 1) * W)
                            dve.wait_ge(qa_ready, 8 * half + m + 1)
                            dve.tensor_tensor(qb[0:2 * HD, j, cols], prep[1][0:2 * HD, :],
                                              qa[0:2 * HD, j, cols].bitcast(F32), ALU.subtract).then_inc(qb_ready, 1)
                        for j in range(J):
                            for i, (t, ck, w) in enumerate(CH):
                                x = len(CH) * j + i
                                dve.wait_ge(max_ps, NCH * half + x + 1)
                                dve.tensor_reduce(k["pmax"][:, j, ck, t:t + 1], mxp[x % 2][:, 0:w], AX.X, ALU.max).then_inc(max_taken, 1)
                        dve.wait_ge(max_taken, 1 + NCH * half + NCH)
                        step.did(dve.tensor_tensor(mx[:], k["pmax"][:, :, 0, :], k["pmax"][:, :, 1, :], ALU.max))
                        step.settle()
                        step.did(dve.tensor_scalar(mcol[:, :, :, 0], mx[:], -1.0, None, ALU.mult))
                        step.settle()
                        dve.scalar_tensor_tensor(out=mcol[:, :, :, 1], in0=mx[:], scalar=-1.0,
                                                 in1=mcol[:, :, :, 0].bitcast(F32), op0=ALU.mult, op1=ALU.subtract).then_inc(mcol_ready, 1)
                        for m in range(2 * J):
                            j, hh = m // 2, m % 2
                            dve.wait_ge(m_turned, 8 * half + m + 1)
                            dve.tensor_copy(qa[2 * HD:2 * HD + 2, j, hh * W:(hh + 1) * W], mxp[m % 2][0:2, :]).then_inc(mrow_ready, 1)
                        for c in range(2):
                            dve.wait_ge(av_done, 1 + NST * half + (4, 12)[c])
                            dve.wait_ge(o_turned, 1 + 2 * half + c)
                            dve.tensor_copy(osb[:], acc[:]).then_inc(o_taken, 1)
                            dve.wait_ge(o_turned, 1 + 2 * half + c + 1)
                            o = otr[:].rearrange("p (i j r) -> p i j r", i=4, j=J)
                            step.did(dve.reciprocal(rcp[:], o[:, :, :, CON]))
                            step.settle()
                            dst = att[:, b * BT + 4 * c:b * BT + 4 * c + 4, bass.ds(g * J * CON, J * CON)]
                            dve.tensor_tensor(dst.rearrange("p i (j r) -> p i j r", j=J), o[:, :, :, 0:CON],
                                              rcp[:].rearrange("p i (j a) -> p i j a", a=1).to_broadcast([P, 4, J, CON]),
                                              ALU.mult).then_inc(att_ready, 1)


def experts(nc, d, k):
    with ExitStack() as ctx:
        def sb(name, shape, dt=F32):
            return ctx.enter_context(nc.sbuf_tensor(name, shape, dt))

        def sem(name):
            return ctx.enter_context(nc.semaphore(name))

        att, h, ident = k["att"], k["h"], k["ident"]
        wo = sb("wo", [P, DC, D])
        attT = sb("attT", [P, DC, B * T])
        stats = sb("stats2", [P, TT, 6])
        mv = sb("mv2", [P, TT, 2])
        ve = sb("ve2", [P, TT])
        sd = sb("sd2", [P, TT])
        rstd = sb("rstd2", [P, TT])
        xn = att
        yT = attT
        yh = k["xh"]
        yl = k["xl"]
        gw = sb("gw", [P, DC, E])
        gu = sb("gu", [P, 2, DC, 2 * F])
        dn = sb("dn", [P, 2, FC, D])
        guh = sb("guh", [P, 2, DC, 2 * F], F32R)
        gul = sb("gul", [P, 2, DC, 2 * F], F32R)
        dnh = sb("dnh", [P, 2, FC, D], F32R)
        dnl = sb("dnl", [P, 2, FC, D], F32R)
        sg = sb("sg", [P, 2, FC, W])
        hm = sb("hm", [P, 2, FC, W])
        hmh = sb("hmh", [P, 2, FC, W], F32R)
        hml = sb("hml", [P, 2, FC, W], F32R)
        R = {n: sb("r_" + n, [P, TT, E]) for n in ("lg", "ex", "p", "eq", "cd", "f1", "f2", "p2", "wd", "cb")}
        S = {n: sb("s_" + n, [P, TT]) for n in ("mx", "sum", "r", "m1", "m2", "c", "w1", "w2", "t")}
        rank = sb("rank", [P, E])
        M = {n: sb("m_" + n, [P, E, E]) for n in ("sim", "ms", "eq", "cd", "map", "id", "t")}
        V = {n: sb("v_" + n, [P, E]) for n in ("pres", "prim", "neg", "bs", "c", "go", "stay")}
        prod = sb("prod", [P, TT, E, E])
        ones = sb("ones", [P, P])
        iot = sb("iot", [P, E])

        ps = [ctx.enter_context(nc.psum_tensor(f"pc{i}", [P, W], F32)) for i in range(8)]

        (wo_in, gw_in, at_turned, at_ready, o_ps, h_ready, var_ready, sd_ready, xn_ready, y_turned, y_full, y_hi, y_lo,
         lg_ps, lg_max, ex_ready, pres_ready, pres_ps, cb_ready, w_split, gu_ps, sg_ready, hm_ready,
         hmh_ready, hml_ready, w_hi, dn_ps, acc_done, dve_step, pool_step, out_done, const2) = (sem(n) for n in (
             "wo_in", "gw_in", "at_turned", "at_ready", "o_ps", "h_ready", "var2_ready", "sd2_ready", "xn2_ready",
             "y_turned", "y_full", "y_hi", "y_lo", "lg_ps", "lg_max", "ex2_ready", "pres_ready", "pres_ps", "cb_ready",
             "w_split", "gu_ps", "sg_ready", "hm_ready", "hmh_ready", "hml_ready", "w_hi", "dn_ps",
             "acc_done", "dve2_step", "pool2_step", "out_done", "const2"))

        ex_in = [sem(f"ex_in{u}") for u in range(2)]

        with nc.Block() as block:
            @block.sync
            def _(sp):
                sp.dma_start(wo[:], d["W_o"].rearrange("(c p) n -> p c n", p=P)).then_inc(wo_in, 16)
                sp.dma_start(gw[:], d["gateT"].rearrange("(c p) e -> p c e", p=P)).then_inc(gw_in, 16)
                sp.dma_start(M["sim"][:].rearrange("p a b -> p (a b)"),
                             d["sim"].rearrange("a b -> (a b)").rearrange("(o n) -> o n", o=1).to_broadcast([P, E * E])).then_inc(gw_in, 16)
                with sp.Fori(0, E // 2) as e2:
                    for u in range(2):
                        e = e2 * 2 + u
                        sp.wait_ge(w_split, 1 + e2 * 2 if u == 0 else e2 * 2)
                        sp.dma_start(gu[:, u], d["guT"][bass.ds(e, 1)].rearrange("o (c p) f -> p (o c) f", p=P)).then_inc(ex_in[u], 16)
                        sp.dma_start(dn[:, u], d["dnT"][bass.ds(e, 1)].rearrange("o (c p) f -> p (o c) f", p=P)).then_inc(ex_in[u], 16)
                sp.wait_ge(acc_done, 1 + E * NW)
                sp.dma_start(d["out"].rearrange("(t p) e -> p t e", p=P), h[:]).then_inc(out_done, 16)
                sp.wait_ge(out_done, 16)

            @block.gpsimd
            def _(pool):
                pool.iota(iot[:], pattern=[[-1, E]], base=E, channel_multiplier=0,
                          allow_small_or_imprecise_dtypes=True).then_inc(pool_step, 1)
                pool.memset(M["id"][:], 0.0).then_inc(pool_step, 1)
                pool.wait_ge(pool_step, 2)
                pool.affine_select(out=M["id"][:], in_=M["id"][:], compare_op=ALU.not_equal, fill=1.0,
                                   base=0, pattern=[[1, E], [-1, E]], channel_multiplier=0).then_inc(const2, 1)
                pool.memset(ones[:], 1.0).then_inc(const2, 1)
                head_start(pool, w_split)
                with pool.Fori(0, E // 2) as e2:
                    for u in range(2):
                        e = e2 * 2 + u
                        pool.wait_ge(w_hi, e + 1)
                        pool.tensor_tensor(gul[:, u], gu[:, u], guh[:, u].bitcast(F32), ALU.subtract)
                        pool.tensor_tensor(dnl[:, u], dn[:, u], dnh[:, u].bitcast(F32), ALU.subtract).then_inc(w_split, 1)

            @block.tensor
            def _(pe):
                for n in range(NW):
                    for c in range(DC):
                        m = n * DC + c
                        if m >= 4:
                            pe.wait_ge(at_ready, m - 3)
                        for i in range(4):
                            last = pe.transpose(ps[m % 4][:, i * P:(i + 1) * P], att[:, 4 * n + i, c * P:(c + 1) * P], ident[:])
                        last.then_inc(at_turned, 1)
                pe.wait_ge(wo_in, 16)
                for t in range(TT):
                    pe.wait_ge(at_ready, (t // 4) * DC + 2)
                    if t >= 4:
                        pe.wait_ge(h_ready, t - 3)
                    for c in range(DC):
                        last = pe.matmul(ps[4 + t % 4][:, 0:D], attT[:, c, t * P:(t + 1) * P], wo[:, c, :], start=(c == 0), stop=(c == DC - 1))
                    last.then_inc(o_ps, 1)
                for n in range(NW):
                    pe.wait_ge(xn_ready, 4 * n + 4)
                    for c in range(DC):
                        m = n * DC + c
                        if m >= 4:
                            pe.wait_ge(y_lo, m - 3)
                        for i in range(4):
                            last = pe.transpose(ps[m % 4][:, i * P:(i + 1) * P], xn[:, 4 * n + i, c * P:(c + 1) * P], ident[:])
                        last.then_inc(y_turned, 1)
                pe.wait_ge(gw_in, 32)
                pe.wait_ge(y_full, NW * DC)
                for t in range(TT):
                    for c in range(DC):
                        last = pe.matmul(ps[4][:, t * E:(t + 1) * E], yT[:, c, t * P:(t + 1) * P], gw[:, c, :], start=(c == 0), stop=(c == DC - 1))
                last.then_inc(lg_ps, 1)
                pe.wait_ge(pres_ready, 1)
                pe.wait_ge(const2, 2)
                pe.matmul(ps[5][:, 0:E], ones[:], V["pres"][:], start=True, stop=True).then_inc(pres_ps, 1)
                pe.wait_ge(cb_ready, 1)
                pe.wait_ge(y_lo, NW * DC)

                def up(e2, u, n):
                    it = e2 * (2 * NW) + u * NW + n
                    cols = slice(n * W, (n + 1) * W)
                    pe.wait_ge(w_split, 1 + e2 * 2 + u + 1)
                    for fc in range(FC):
                        pe.wait_ge(hm_ready, 1 + it * FC if fc == 0 else it * FC)
                        for s in range(2):
                            f = slice(s * F + fc * P, s * F + (fc + 1) * P)
                            for c in range(DC):
                                last = three(pe, ps[2 * fc + s][:], (guh[:, u, c, f], gul[:, u, c, f]),
                                             (yh[:, c, cols], yl[:, c, cols]), c == 0, c == DC - 1)
                        last.then_inc(gu_ps, 1)

                def down(e2, u, n):
                    it = e2 * (2 * NW) + u * NW + n
                    r = n % 2
                    pe.wait_ge(hml_ready, it * FC + FC)
                    for i in range(4):
                        pe.wait_ge(acc_done, 1 + it)
                        tok = slice(i * P, (i + 1) * P)
                        for fc in range(FC):
                            last = three(pe, ps[4 + i][:, 0:D], (hmh[:, r, fc, tok], hml[:, r, fc, tok]),
                                         (dnh[:, u, fc, :], dnl[:, u, fc, :]), fc == 0, fc == FC - 1)
                        last.then_inc(dn_ps, 1)

                head_start(pe, dn_ps)
                with pe.Fori(0, E // 2) as e2:
                    for u in range(2):
                        for n in range(NW):
                            up(e2, u, n)
                            down(e2, u, n)

            @block.scalar
            def _(act):
                def high_weights(e2, u):
                    act.wait_ge(ex_in[u], e2 * 32 + 32)
                    act.wait_ge(dn_ps, 1 + e2 * (2 * 4 * NW))
                    act.activation(guh[:, u], gu[:, u], ACT.Copy)
                    act.activation(dnh[:, u], dn[:, u], ACT.Copy).then_inc(w_hi, 1)

                for n in range(NW):
                    for c in range(DC):
                        m = n * DC + c
                        act.wait_ge(at_turned, m + 1)
                        act.activation(attT[:, c, n * W:(n + 1) * W], ps[m % 4][:], ACT.Copy).then_inc(at_ready, 1)
                act.wait_ge(var_ready, 1)
                act.activation(sd[:], ve[:], ACT.Sqrt).then_inc(sd_ready, 1)
                act.wait_ge(o_ps, TT)
                for n in range(NW):
                    for c in range(DC):
                        m = n * DC + c
                        cols = slice(n * W, (n + 1) * W)
                        act.wait_ge(y_turned, m + 1)
                        act.activation(yT[:, c, cols], ps[m % 4][:], ACT.Copy).then_inc(y_full, 1)
                        act.activation(yh[:, c, cols], ps[m % 4][:], ACT.Copy).then_inc(y_hi, 1)
                act.wait_ge(lg_max, 1)
                act.activation(R["ex"][:], R["lg"][:], ACT.Exp).then_inc(ex_ready, 1)
                with act.Fori(0, E // 2) as e2:
                    high_weights(e2, 0)
                    high_weights(e2, 1)
                    for u in range(2):
                        for n in range(NW):
                            it = e2 * (2 * NW) + u * NW + n
                            r = n % 2
                            for fc in range(FC):
                                act.wait_ge(gu_ps, it * FC + fc + 1)
                                act.activation(sg[:, r, fc, :], ps[2 * fc][:], ACT.Silu).then_inc(sg_ready, 1)
                            for fc in range(FC):
                                act.wait_ge(hm_ready, 1 + it * FC + fc + 1)
                                act.activation(hmh[:, r, fc, :], hm[:, r, fc, :], ACT.Copy).then_inc(hmh_ready, 1)

            @block.vector
            def _(dve):
                step = Chain(dve, dve_step)

                def did(ins):
                    step.did(ins)
                    step.settle()

                for t in range(TT):
                    dve.wait_ge(o_ps, t + 1)
                    dve.tensor_tensor(h[:, t, :], h[:, t, :], ps[4 + t % 4][:, 0:D], ALU.add).then_inc(h_ready, 1)
                dve.wait_ge(h_ready, TT)
                for t in range(TT):
                    step.did(dve.bn_stats(stats[:, t, :], h[:, t, :]))
                step.settle()
                for t in range(TT):
                    step.did(dve.bn_aggr(mv[:, t, :], stats[:, t, :]))
                step.settle()
                dve.tensor_scalar(ve[:], mv[:, :, 1], 1e-5, None, ALU.add).then_inc(var_ready, 1)
                dve.wait_ge(sd_ready, 1)
                did(dve.reciprocal(rstd[:], sd[:]))
                dve.wait_ge(at_turned, NW * DC)
                for t in range(TT):
                    dve.tensor_scalar(xn[:, t, :], h[:, t, :], mv[:, t, 0:1], rstd[:, t:t + 1],
                                      ALU.subtract, ALU.mult).then_inc(xn_ready, 1)
                for n in range(NW):
                    for c in range(DC):
                        m = n * DC + c
                        cols = slice(n * W, (n + 1) * W)
                        dve.wait_ge(y_hi, m + 1)
                        dve.tensor_tensor(yl[:, c, cols], ps[m % 4][:], yh[:, c, cols].bitcast(F32), ALU.subtract).then_inc(y_lo, 1)

                def wide(s):
                    return S[s][:].rearrange("p (t a) -> p t a", a=1).to_broadcast([P, TT, E])

                def each(v):
                    return v[:].rearrange("p (a e) -> p a e", a=1).to_broadcast([P, TT, E])

                dve.wait_ge(lg_ps, 1)
                lg = ps[4][:, 0:TT * E].rearrange("p (t e) -> p t e", e=E)
                did(dve.tensor_reduce(S["mx"][:], lg, AX.X, ALU.max))
                dve.tensor_tensor(R["lg"][:], lg, wide("mx"), ALU.subtract).then_inc(lg_max, 1)
                dve.wait_ge(ex_ready, 1)
                did(dve.tensor_reduce(S["sum"][:], R["ex"][:], AX.X, ALU.add))
                did(dve.reciprocal(S["r"][:], S["sum"][:]))
                did(dve.tensor_tensor(R["p"][:], R["ex"][:], wide("r"), ALU.mult))
                dve.wait_ge(const2, 2)

                def largest(src, m, f):
                    did(dve.tensor_reduce(S[m][:], R[src][:], AX.X, ALU.max))
                    did(dve.tensor_tensor(R["eq"][:], R[src][:], wide(m), ALU.is_equal))
                    did(dve.tensor_tensor(R["cd"][:], R["eq"][:], each(iot), ALU.mult))
                    did(dve.tensor_reduce(S["c"][:], R["cd"][:], AX.X, ALU.max))
                    did(dve.tensor_tensor(R[f][:], each(iot), wide("c"), ALU.is_equal))

                largest("p", "m1", "f1")
                did(dve.scalar_tensor_tensor(out=R["p2"][:], in0=R["f1"][:], scalar=-2.0, in1=R["p"][:], op0=ALU.mult, op1=ALU.add))
                dve.tensor_reduce(V["pres"][:], R["f1"][:].rearrange("p t e -> p e t"), AX.X, ALU.add).then_inc(pres_ready, 1)
                largest("p2", "m2", "f2")
                did(dve.tensor_tensor(S["t"][:], S["m1"][:], S["m2"][:], ALU.add))
                did(dve.tensor_scalar(S["t"][:], S["t"][:], 1e-12, None, ALU.max))
                did(dve.reciprocal(S["r"][:], S["t"][:]))
                did(dve.tensor_tensor(S["w1"][:], S["m1"][:], S["r"][:], ALU.mult))
                did(dve.tensor_tensor(S["w2"][:], S["m2"][:], S["r"][:], ALU.mult))
                did(dve.tensor_tensor(R["wd"][:], R["f1"][:], wide("w1"), ALU.mult))
                did(dve.tensor_tensor(R["cd"][:], R["f2"][:], wide("w2"), ALU.mult))
                did(dve.tensor_tensor(R["wd"][:], R["wd"][:], R["cd"][:], ALU.add))
                def over_i(v):
                    return v[:].rearrange("p (a e) -> p a e", a=1).to_broadcast([P, E, E])

                def over_j(v):
                    return v[:].rearrange("p (e a) -> p e a", a=1).to_broadcast([P, E, E])

                dve.wait_ge(pres_ps, 1)
                dve.wait_ge(gw_in, 32)
                did(dve.tensor_scalar(V["prim"][:], ps[5][:, 0:E], 0.5, None, ALU.is_ge))
                did(dve.tensor_scalar(V["neg"][:], V["prim"][:], -LOWEST, LOWEST, ALU.mult, ALU.add))
                did(dve.tensor_tensor(M["ms"][:], M["sim"][:], over_i(V["prim"]), ALU.mult))
                did(dve.tensor_tensor(M["ms"][:], M["ms"][:], over_i(V["neg"]), ALU.add))
                did(dve.tensor_reduce(V["bs"][:], M["ms"][:], AX.X, ALU.max))
                did(dve.tensor_tensor(M["eq"][:], M["ms"][:], over_j(V["bs"]), ALU.is_equal))
                did(dve.tensor_tensor(M["cd"][:], M["eq"][:], over_i(iot), ALU.mult))
                did(dve.tensor_reduce(V["c"][:], M["cd"][:], AX.X, ALU.max))
                did(dve.tensor_tensor(M["map"][:], over_i(iot), over_j(V["c"]), ALU.is_equal))
                did(dve.tensor_scalar(V["go"][:], V["bs"][:], 0.7, None, ALU.is_ge))
                did(dve.tensor_tensor(V["go"][:], V["go"][:], V["prim"][:], ALU.is_gt))
                did(dve.tensor_scalar(V["stay"][:], V["go"][:], -1.0, 1.0, ALU.mult, ALU.add))
                did(dve.tensor_tensor(M["map"][:], M["map"][:], over_j(V["go"]), ALU.mult))
                did(dve.tensor_tensor(M["t"][:], M["id"][:], over_j(V["stay"]), ALU.mult))
                did(dve.tensor_tensor(M["map"][:], M["map"][:], M["t"][:], ALU.add))
                for j in range(E):
                    step.did(dve.tensor_tensor(prod[:, :, j, :], R["wd"][:], M["map"][:, :, j].rearrange("p (a e) -> p a e", a=1).to_broadcast([P, TT, E]), ALU.mult))
                step.settle()
                dve.tensor_reduce(R["cb"][:], prod[:], AX.X, ALU.add).then_inc(cb_ready, 1)
                dve.wait_ge(cb_ready, 1)

                head_start(dve, hm_ready, acc_done)
                with dve.Fori(0, E // 2) as e2:
                    for u in range(2):
                        for n in range(NW):
                            it = e2 * (2 * NW) + u * NW + n
                            r = n % 2
                            for fc in range(FC):
                                dve.wait_ge(sg_ready, it * FC + fc + 1)
                                dve.tensor_tensor(hm[:, r, fc, :], sg[:, r, fc, :], ps[2 * fc + 1][:], ALU.mult).then_inc(hm_ready, 1)
                            for fc in range(FC):
                                dve.wait_ge(hmh_ready, it * FC + fc + 1)
                                dve.tensor_tensor(hml[:, r, fc, :], hm[:, r, fc, :], hmh[:, r, fc, :].bitcast(F32), ALU.subtract).then_inc(hml_ready, 1)
                            for i in range(4):
                                t = 4 * n + i
                                dve.wait_ge(dn_ps, 1 + it * 4 + i + 1)
                                last = dve.scalar_tensor_tensor(out=h[:, t, :], in0=ps[4 + i][:, 0:D],
                                                                scalar=R["cb"][:, t, bass.ds(e2 * 2 + u, 1)], in1=h[:, t, :],
                                                                op0=ALU.mult, op1=ALU.add)
                            last.then_inc(acc_done, 1)


def tower(nc, d):
    with ExitStack() as ctx:
        def sb(name, shape, dt=F32):
            return ctx.enter_context(nc.sbuf_tensor(name, shape, dt))

        k = {
            "h": sb("h", [P, TT, D]),
            "cos": sb("cos", [P, BT, ROPE]), "sin": sb("sin", [P, BT, ROPE]),
            "ident": sb("ident", [P, P]), "ident_r": sb("ident_r", [P, P], F32R),
            "mask_qk": sb("mask_qk", [P, P], F32R), "mask_kq": sb("mask_kq", [P, P], F32R),
            "xh": sb("xh", [P, DC, B * T], F32R), "xl": sb("xl", [P, DC, B * T], F32R),
            "pmax": sb("pmax", [P, J, 2, BT]),
        }
        with ExitStack() as inner:
            def sbi(name, shape, dt=F32):
                return inner.enter_context(nc.sbuf_tensor(name, shape, dt))

            att = sb("att", [P, TT, D])
            k.update({
                "qh": sbi("qh", [P, B * T], F32R), "ql": sbi("ql", [P, B * T], F32R), "kv": sbi("kv", [P, B * T], F32R),
                "wkrh": sbi("wkrh", [P, DC, HEADS * ROPE], F32R), "wkrl": sbi("wkrl", [P, DC, HEADS * ROPE], F32R),
                "wqxh": sbi("wqxh", [P, G, J * HD], F32R), "wqxl": sbi("wqxl", [P, G, J * HD], F32R),
                "wkxh": sbi("wkxh", [P, G, 2 * J * CON], F32R), "wkxl": sbi("wkxl", [P, G, 2 * J * CON], F32R),
                "vst": sbi("vst", [P, BT, J, 32]),
                "kst": sbi("kst", [2 * HD + 2, J, T], F32R),
                "att": att,
            })
            k["ones_rows"] = k["kst"][2 * HD:2 * HD + 2, :, :]
            prepare(nc, d, k)
            k["qa"] = sbi("qa", [2 * HD + 2, J, T], F32R)
            k["qb"] = sbi("qb", [2 * HD, J, T], F32R)
            attention(nc, k)
        experts(nc, d, k)


_WEIGHTS = ['L0_tok_W1', 'L0_tok_b1', 'L0_tok_W2', 'L0_tok_b2', 'L0_attn_W_kv', 'L0_attn_g_kv', 'L0_attn_W_kdec',
            'L0_attn_W_vdec', 'L0_attn_W_q', 'L0_attn_W_qdec', 'L0_attn_W_krope', 'L0_attn_W_qrope', 'L0_attn_W_o']


def kernel(**inputs):
    import numpy as np
    import concourse.bacc as bacc
    from concourse.bass_utils import run_bass_kernel_spmd

    nc = bacc.Bacc("TRN2", target_bir_lowering=False, num_devices=1, dynamic_dma_scratch_size=1024)
    nc.disable_value_cache = True
    x = np.asarray(inputs["x"])
    tokens = x.reshape(B * T, D)
    arrays = {n.split("_", 2)[2]: np.ascontiguousarray(inputs[n]) for n in _WEIGHTS}
    arrays["x"] = np.ascontiguousarray(tokens)
    arrays["xT"] = np.ascontiguousarray(tokens.T)
    arrays["gateT"] = np.ascontiguousarray(np.asarray(inputs["L0_ffn_gate_weight"]).T)
    arrays["guT"] = np.ascontiguousarray(np.asarray(inputs["L0_ffn_gate_up_proj"]).transpose(0, 2, 1))
    arrays["dnT"] = np.ascontiguousarray(np.asarray(inputs["L0_ffn_down_proj"]).transpose(0, 2, 1))
    arrays["sim"] = np.ascontiguousarray(inputs["L0_ffn_similarity_matrix"])
    inv_freq = 1.0 / 10000.0 ** (np.arange(0, ROPE, 2, dtype=np.float32) / ROPE)
    freqs = np.outer(np.arange(T, dtype=np.float32), inv_freq)
    arrays["cos"] = np.cos(np.concatenate([freqs, freqs], -1)).astype(np.float32)
    arrays["sin"] = np.sin(np.concatenate([-freqs, freqs], -1)).astype(np.float32)

    d = {n: nc.dram_tensor("in_" + n, a.shape, mybir.dt.from_np(a.dtype), kind="ExternalInput").ap()
         for n, a in arrays.items()}
    d["out"] = nc.dram_tensor("out_h", (B * T, D), F32, kind="ExternalOutput").ap()
    tower(nc, d)
    r = run_bass_kernel_spmd(nc, [{"in_" + n: a for n, a in arrays.items()}], core_ids=[0])
    return r.results[0]["out_h"].reshape(B, T, D)
```

```python
from contextlib import ExitStack

import concourse.bass as bass
from concourse import mybir

F32 = mybir.dt.float32
F32R = mybir.dt.float32r
BF16 = mybir.dt.bfloat16
ALU = mybir.AluOpType
ACT = mybir.ActivationFunctionType
AX = mybir.AxisListType

P = 128
B, T, D = 2, 1024, 256
TT = B * T // P
BT = T // P
DC = D // P
HEADS, CON, ROPE = 16, 16, 32
HD = CON + ROPE
J = 4
G = HEADS // J
KVR, QR = 64, 128
E, F = 8, 256
FC = F // P
TOKH = 128
W = 512
FULL = 256
NW = B * T // W
BIG = float(2 ** 100)
LOWEST = -3.0e38


class Chain:

    def __init__(self, eng, sem, base=0):
        self.eng, self.sem, self.base, self.n = eng, sem, base, 0

    def did(self, ins):
        self.n += 1
        ins.then_inc(self.sem, 1)
        return ins

    def settle(self):
        self.eng.wait_ge(self.sem, self.base + self.n)


def head_start(eng, *sems):
    for s in sems:
        eng.sem_inc(s, 1)


def three(pe, out, stat, mov, first=True, last=True):
    (sh, sl), (mh, ml) = stat, mov
    pe.matmul(out, sh, mh, start=first, stop=False)
    pe.matmul(out, sh, ml, start=False, stop=False)
    return pe.matmul(out, sl, mh, start=False, stop=last)


def prepare(nc, d, k):
    with ExitStack() as ctx:
        def sb(name, shape, dt=F32):
            return ctx.enter_context(nc.sbuf_tensor(name, shape, dt))

        def sem(name):
            return ctx.enter_context(nc.semaphore(name))

        xT = sb("xT", [P, DC, B * T])
        xin = sb("xin", [P, TT, D])
        w1 = sb("w1", [P, DC, TOKH])
        w2 = sb("w2", [P, 1])
        b1 = sb("b1", [P, 1])
        b2 = sb("b2", [P, 1])
        hid = sb("hid", [P, 2, W])
        en = sb("en", [P, TT])
        de = sb("de", [P, TT])
        ex = sb("ex", [P, TT])
        rs = sb("rs", [P, TT])
        wt = sb("wt", [P, TT])
        stats = sb("stats", [P, TT, 6])
        mv = sb("mv", [P, TT, 2])
        ve = sb("ve", [P, TT])
        sd = sb("sd", [P, TT])
        rstd = sb("rstd", [P, TT])
        xn = xin
        wq = sb("wq", [P, DC, QR])
        wkv = sb("wkv", [P, DC, KVR])
        gkv = sb("gkv", [P, KVR])
        kvsq = sb("kvsq", [P, TT, KVR])
        kvn = sb("kvn", [P, TT, KVR])
        kvd = sb("kvd", [P, TT, 2 * KVR])
        kvm = sb("kvm", [P, TT])
        kvs = sb("kvs", [P, TT])
        kvr = sb("kvr", [P, TT])
        kvhi = sb("kvhi", [P, 2, W], F32R)
        wkr, wqx, wkx = k["wkr"], k["wqx"], k["wkx"]
        lowrow = sb("lowrow", [P, 1])
        mask1 = sb("mask1", [P, P])
        mask2 = sb("mask2", [P, P])

        ps = [ctx.enter_context(nc.psum_tensor(f"pa{i}", [P, W], F32)) for i in range(8)]

        xT_in, x_in, tok_w_in, low_w_in, dec_w_in, tab_in = (sem(n) for n in (
            "xT_in",
            "x_in", "tok_w_in", "low_w_in", "dec_w_in", "tab_in"))
        hid_ps, hid_ready, en_ps = sem("hid_ps"), sem("hid_ready"), sem("en_ps")
        diff_ready, exp_ready, var_ready, sd_ready = (sem(n) for n in ("diff_ready", "exp_ready", "var_ready", "sd_ready"))
        xn_ready, turned, xn_turned = (sem(n) for n in ("xn_ready", "turned", "xn_turned"))
        const_ready, kv_ps, kv_sq, kv_mean, kv_sd = (sem(n) for n in (
            "const_ready", "kv_ps", "kv_sq", "kv_mean", "kv_sd"))
        qc_ps, qc_ready = sem("qc_ps"), sem("qc_ready")
        kvn_ready, kv_turned, kv_hi, kv_split = sem("kvn_ready"), sem("kv_turned"), sem("kv_hi"), sem("kv_split")
        dve_step, pool_step, mask_in = sem("dve_step"), sem("pool_step"), sem("mask_in")

        with nc.Block() as block:
            @block.sync
            def _(sp):
                for c in range(DC):
                    sp.dma_start(xT[:, c, :], d["xT"][c * P:(c + 1) * P, :]).then_inc(xT_in, 16)
                sp.dma_start(w1[:], d["W1"].rearrange("(c p) h -> p c h", p=P)).then_inc(tok_w_in, 16)
                sp.dma_start(b1[:], d["b1"].rearrange("(p a) -> p a", a=1)).then_inc(tok_w_in, 16)
                sp.dma_start(w2[:], d["W2"]).then_inc(tok_w_in, 16)
                sp.dma_start(b2[:], d["b2"].rearrange("(p a) -> p a", a=1).to_broadcast([P, 1])).then_inc(tok_w_in, 16)
                sp.dma_start(xin[:], d["x"].rearrange("(t p) e -> p t e", p=P)).then_inc(x_in, 16)
                sp.dma_start(wq[:], d["W_q"].rearrange("(c p) r -> p c r", p=P)).then_inc(low_w_in, 16)
                sp.dma_start(wkv[:], d["W_kv"].rearrange("(c p) r -> p c r", p=P)).then_inc(low_w_in, 16)
                sp.dma_start(gkv[:], d["g_kv"].rearrange("(a r) -> a r", a=1).to_broadcast([P, KVR])).then_inc(low_w_in, 16)
                sp.dma_start(wkr[:], d["W_krope"].rearrange("(c p) n -> p c n", p=P)).then_inc(dec_w_in, 16)
                sp.dma_start(wqx[:, :, 0:J * ROPE], d["W_qrope"].rearrange("p (g n) -> p g n", g=G)).then_inc(dec_w_in, 16)
                sp.dma_start(wqx[:, :, J * ROPE:J * HD], d["W_qdec"].rearrange("p (g n) -> p g n", g=G)).then_inc(dec_w_in, 16)
                for r in range(2):
                    rows = slice(r * KVR, (r + 1) * KVR)
                    sp.dma_start(wkx[rows, :, 0:J * CON], d["W_kdec"].rearrange("p (g n) -> p g n", g=G)).then_inc(dec_w_in, 16)
                    sp.dma_start(wkx[rows, :, J * CON:], d["W_vdec"].rearrange("p (g n) -> p g n", g=G)).then_inc(dec_w_in, 16)
                sp.dma_start(k["cos"][:], d["cos"].rearrange("(t p) r -> p t r", p=P)).then_inc(tab_in, 16)
                sp.dma_start(k["sin"][:], d["sin"].rearrange("(t p) r -> p t r", p=P)).then_inc(tab_in, 16)
                sp.wait_ge(tab_in, 32)

            @block.gpsimd
            def _(pool):
                step = Chain(pool, pool_step)
                step.did(pool.memset(k["ident"][:], 0.0))
                step.did(pool.memset(mask1[:], 0.0))
                step.did(pool.memset(mask2[:], 0.0))
                step.did(pool.memset(lowrow[:], -1.0))
                step.settle()
                step.did(pool.affine_select(out=k["ident"][:], in_=k["ident"][:], compare_op=ALU.not_equal, fill=1.0,
                                            base=0, pattern=[[-1, P]], channel_multiplier=1))
                step.did(pool.affine_select(out=mask1[:], in_=mask1[:], compare_op=ALU.is_ge, fill=-BIG,
                                            base=0, pattern=[[-1, P]], channel_multiplier=1))
                step.did(pool.affine_select(out=mask2[:], in_=mask2[:], compare_op=ALU.is_ge, fill=-BIG,
                                            base=0, pattern=[[1, P]], channel_multiplier=-1))
                step.did(pool.memset(lowrow[0:KVR, :], 0.0))
                step.settle()
                pool.tensor_copy(k["ident_b"][:], k["ident"][:])
                pool.tensor_copy(k["mask_qk"][:], mask1[:])
                pool.tensor_copy(k["mask_kq"][:], mask2[:]).then_inc(const_ready, 1)
                step.did(pool.memset(k["vst"][:], 0.0))
                step.settle()
                step.did(pool.memset(k["vst"][:, :, :, :, CON:CON + 1], 1.0))
                step.settle()

            def energies(pe, n):
                pe.wait_ge(hid_ready, n + 1)
                for i in range(4):
                    t = 4 * n + i
                    last = pe.matmul(ps[2][:, t:t + 1], hid[:, n % 2, i * P:(i + 1) * P], w2[:], start=True, stop=True)
                last.then_inc(en_ps, 1)

            @block.tensor
            def _(pe):
                pe.wait_ge(xT_in, 32)
                pe.wait_ge(tok_w_in, 64)
                for n in range(NW):
                    if n >= 2:
                        pe.wait_ge(hid_ready, n - 1)
                    for c in range(DC):
                        last = pe.matmul(ps[n % 2][:], w1[:, c, :], xT[:, c, n * W:(n + 1) * W],
                                         start=(c == 0), stop=(c == DC - 1))
                    last.then_inc(hid_ps, 1)
                    if n >= 1:
                        energies(pe, n - 1)
                energies(pe, NW - 1)
                pe.wait_ge(const_ready, 1)
                for n in range(NW):
                    pe.wait_ge(xn_ready, 4 * n + 4)
                    for c in range(DC):
                        m = n * DC + c
                        if m >= 4:
                            pe.wait_ge(xn_turned, m - 3)
                        for i in range(4):
                            last = pe.transpose(ps[4 + m % 4][:, i * P:(i + 1) * P],
                                                xn[:, 4 * n + i, c * P:(c + 1) * P], k["ident"][:])
                        last.then_inc(turned, 1)
                pe.wait_ge(low_w_in, 48)
                for n in range(NW):
                    pe.wait_ge(xn_turned, DC * n + 2)
                    cols = slice(n * W, (n + 1) * W)
                    for t in range(4 * n, 4 * n + 4):
                        tok = slice(t * P, (t + 1) * P)
                        out = ps[2 + t // 8][:, (t % 8) * KVR:(t % 8 + 1) * KVR]
                        if t == 0:
                            pe.wait_ge(diff_ready, 1)
                        for c in range(DC):
                            last = pe.matmul(out, k["xn"][:, c, tok], wkv[:, c, :], start=(c == 0), stop=(c == DC - 1))
                    last.then_inc(kv_ps, 1)
                    if n >= 2:
                        pe.wait_ge(qc_ready, n - 1)
                    for c in range(DC):
                        last = pe.matmul(ps[n % 2][:], wq[:, c, :], k["xn"][:, c, cols], start=(c == 0), stop=(c == DC - 1))
                    last.then_inc(qc_ps, 1)
                pe.wait_ge(kvn_ready, 1)
                for n in range(NW):
                    for i in range(4):
                        last = pe.transpose(ps[4 + n][:, i * P:(i + 1) * P], kvd[:, 4 * n + i], k["ident"][:])
                    last.then_inc(kv_turned, 1)

            @block.scalar
            def _(act):
                act.wait_ge(tok_w_in, 64)
                for n in range(NW):
                    act.wait_ge(hid_ps, n + 1)
                    if n >= 2:
                        act.wait_ge(en_ps, n - 1)
                    act.activation(hid[:, n % 2, :], ps[n % 2][:], ACT.Tanh, bias=b1[:, 0:1]).then_inc(hid_ready, 1)
                act.wait_ge(diff_ready, 1)
                act.activation(ex[:], de[:], ACT.Exp).then_inc(exp_ready, 1)
                act.wait_ge(var_ready, 1)
                act.activation(sd[:], ve[:], ACT.Sqrt).then_inc(sd_ready, 1)
                for n in range(NW):
                    for c in range(DC):
                        m = n * DC + c
                        act.wait_ge(turned, m + 1)
                        act.activation(k["xn"][:, c, n * W:(n + 1) * W], ps[4 + m % 4][:], ACT.Copy).then_inc(xn_turned, 1)
                for n in range(NW):
                    act.wait_ge(qc_ps, n + 1)
                    act.activation(k["qc"][:, n * W:(n + 1) * W], ps[n % 2][:], ACT.Copy).then_inc(qc_ready, 1)
                for r in range(2):
                    act.wait_ge(kv_ps, 2 * r + 2)
                    act.activation(kvsq[:, 8 * r:8 * r + 8, :].rearrange("p t r -> p (t r)"), ps[2 + r][:],
                                   ACT.Square).then_inc(kv_sq, 1)
                act.wait_ge(kv_mean, 1)
                act.activation(kvs[:], kvm[:], ACT.Sqrt).then_inc(kv_sd, 1)
                for n in range(NW):
                    act.wait_ge(kv_turned, n + 1)
                    if n >= 2:
                        act.wait_ge(kv_split, n - 1)
                    act.activation(kvhi[:, n % 2, :], ps[4 + n][:], ACT.Copy).then_inc(kv_hi, 1)

            @block.vector
            def _(dve):
                step = Chain(dve, dve_step)
                dve.memset(k["ones_rows"].bitcast(F32), 1.0)
                dve.memset(k["pmax"][:], LOWEST)
                dve.wait_ge(tok_w_in, 64)
                dve.wait_ge(en_ps, NW)
                step.did(dve.tensor_scalar(en[:], ps[2][:, 0:TT], b2[:, 0:1], None, ALU.add))
                step.settle()
                dve.tensor_tensor(de[:], en[:], en[:], ALU.subtract).then_inc(diff_ready, 1)
                dve.wait_ge(exp_ready, 1)
                step.did(dve.reciprocal(rs[:], ex[:]))
                step.settle()
                step.did(dve.tensor_tensor(wt[:], ex[:], rs[:], ALU.mult))
                dve.wait_ge(x_in, 16)
                step.settle()
                for t in range(TT):
                    step.did(dve.tensor_scalar(k["h"][:, t, :], xin[:, t, :], wt[:, t:t + 1], None, ALU.mult))
                step.settle()
                for t in range(TT):
                    step.did(dve.bn_stats(stats[:, t, :], k["h"][:, t, :]))
                step.settle()
                for t in range(TT):
                    step.did(dve.bn_aggr(mv[:, t, :], stats[:, t, :]))
                step.settle()
                dve.tensor_scalar(ve[:], mv[:, :, 1], 1e-5, None, ALU.add).then_inc(var_ready, 1)
                dve.wait_ge(sd_ready, 1)
                step.did(dve.reciprocal(rstd[:], sd[:]))
                step.settle()
                for t in range(TT):
                    dve.tensor_scalar(xn[:, t, :], k["h"][:, t, :], mv[:, t, 0:1], rstd[:, t:t + 1],
                                      ALU.subtract, ALU.mult).then_inc(xn_ready, 1)
                dve.wait_ge(kv_sq, 2)
                step.did(dve.tensor_reduce(kvr[:], kvsq[:], AX.X, ALU.add))
                step.settle()
                dve.tensor_scalar(kvm[:], kvr[:], 1.0 / KVR, 1e-6, ALU.mult, ALU.add).then_inc(kv_mean, 1)
                dve.wait_ge(kv_sd, 1)
                step.did(dve.reciprocal(kvr[:], kvs[:]))
                step.settle()
                for r in range(2):
                    step.did(dve.tensor_tensor(
                        kvn[:, 8 * r:8 * r + 8, :], ps[2 + r][:].rearrange("p (t r) -> p t r", r=KVR),
                        kvr[:, 8 * r:8 * r + 8].rearrange("p (t a) -> p t a", a=1).to_broadcast([P, 8, KVR]), ALU.mult))
                step.settle()
                for r in range(2):
                    last = dve.tensor_tensor(kvd[:, :, r * KVR:(r + 1) * KVR], kvn[:],
                                             gkv[:].rearrange("p (a r) -> p a r", a=1).to_broadcast([P, TT, KVR]), ALU.mult)
                last.then_inc(kvn_ready, 1)
                dve.wait_ge(const_ready, 1)
                for n in range(NW):
                    dve.wait_ge(kv_hi, n + 1)
                    dve.scalar_tensor_tensor(out=kvtmp(k, n), in0=kvhi[:, n % 2, :].bitcast(F32), scalar=lowrow[:, 0:1],
                                             in1=ps[4 + n][:], op0=ALU.mult, op1=ALU.add).then_inc(kv_split, 1)


def kvtmp(k, n):
    return k["kv"][:, n * W:(n + 1) * W]


def chunks():
    for t in range(BT):
        for ck in range(t // 4 + 1):
            yield t, ck, min(W, (t + 1) * P - ck * W)


def steps():
    for c in range(BT // 4):
        for kt in range(4 * c + 4):
            yield c, kt, max(0, kt - 4 * c) * P


CH = list(chunks())
ST = list(steps())
NC, NS = len(CH), len(ST)
RAWS = 4
PROBS = 4
TILES = ((0, 3), (3, 6), (6, 8), (8, 8))


def slot(tiles):
    first_x, x = 2, 0
    share = {7: 2, 8: 2}
    where = dict(zip((2, 5, 8), range(*tiles)))
    for u in range(NS):
        yield "S", u
        if u < 2:
            yield "T", u
        if u in where:
            yield "P", where[u]
        if u >= first_x:
            for _ in range(share.get(u, 1)):
                yield "X", x
                x += 1
        if u:
            yield "V", u - 1
    yield "V", NS - 1
    yield "M", 0
    yield "O", 0


def slots(g, last):
    for b in range(B):
        half = g * 2 + b
        final = last and b == B - 1
        for j in range(J):
            more = not (final and j == J - 1)
            tiles = (0, 0) if final else TILES[j]
            ev = [e for e in slot(tiles) if more or e[0] not in "TXM"]
            yield half * J + j, half, j, b, ev


def attention(nc, k):
    with ExitStack() as ctx:
        def sb(name, shape, dt=F32):
            return ctx.enter_context(nc.sbuf_tensor(name, shape, dt))

        def sem(name):
            return ctx.enter_context(nc.semaphore(name))

        SCALE = float(1.0 / (float(HD) ** 0.5))
        raw = sb("raw", [P, RAWS, 7 * J * CON])
        roc = sb("roc", [P, 2, 2 * J, ROPE])
        ros = sb("ros", [P, 2, 2 * J, ROPE])
        kraw = sb("kraw", [P, 2, J, HD])
        qd = sb("qd", [P, 2, BT, J, 2, HD])
        khl = sb("khl", [P, 2, BT, J, 2, HD], F32R)
        prob = sb("prob", [P, PROBS, W])
        mx = sb("mx", [P, 2, BT])
        mcol = sb("mcol", [P, 2, BT, 2], F32R)
        osb = sb("osb", [P, 2 * P])
        rcp = sb("rcp", [P, BT])
        kst, qa, qb = k["kst"], k["qa"], k["qb"]
        xn, qc, kv, vst, att = (k[n] for n in ("xn", "qc", "kv", "vst", "att"))
        ident, ident_b, mask_qk, mask_kq = (k[n] for n in ("ident", "ident_b", "mask_qk", "mask_kq"))

        prep = [ctx.enter_context(nc.psum_tensor(f"prep{i}", [P, W], F32)) for i in range(2)]
        mxp = [ctx.enter_context(nc.psum_tensor(f"mxp{i}", [P, W], F32)) for i in range(2)]
        sc = [ctx.enter_context(nc.psum_tensor(f"sc{i}", [P, W], F32)) for i in range(2)]
        acc = ctx.enter_context(nc.psum_tensor("acc", [P, W], F32))
        otr = ctx.enter_context(nc.psum_tensor("otr", [P, W], F32))

        (proj_done, raw_ready, arr_ready, k_turned, q_turned, kst_ready, qa_ready, qb_ready, max_ps, max_taken,
         mcol_ready, m_turned, mrow_ready, score_ps, exp_done, av_done, o_taken, o_turned, att_ready,
         pool_step, dve_step, o_step) = (sem(n) for n in (
             "proj_done", "raw_ready", "arr_ready", "k_turned", "q_turned", "kst_ready", "qa_ready", "qb_ready",
             "max_ps", "max_taken", "mcol_ready", "m_turned", "mrow_ready", "score_ps", "exp_done", "av_done",
             "o_taken", "o_turned", "att_ready", "at_pool_step", "at_dve_step", "o_step"))

        def next_half(g, b):
            return (g, 1) if b == 0 else (g + 1, 0)

        with nc.Block() as block:
            @block.tensor
            def _(pe):
                def project(g, b, n, t, turned):
                    if t >= 2:
                        pe.wait_ge(raw_ready, n * BT + (t - 1))
                    if turned is not None:
                        pe.wait_ge(kst_ready, 1 + turned)
                        pe.wait_ge(qb_ready, 1 + turned)
                    out = prep[t % 2]
                    tok = slice((b * BT + t) * P, (b * BT + t + 1) * P)
                    cols = bass.ds(g * J * ROPE, J * ROPE)
                    for c in range(DC):
                        pe.matmul(out[:, 0:J * ROPE], xn[:, c, tok], k["wkr"][:, c, cols], start=(c == 0), stop=(c == DC - 1))
                    pe.matmul(out[:, J * ROPE:J * (ROPE + HD)], qc[:, tok], k["wqx"][:, bass.ds(g, 1), :], start=True, stop=True)
                    pe.matmul(out[:, J * (ROPE + HD):7 * J * CON], kv[:, tok].bitcast(F32), k["wkx"][:, bass.ds(g, 1), :],
                              start=True, stop=True).then_inc(proj_done, 1)

                def turn(hd, j, b, hh, projected):
                    pe.wait_ge(raw_ready, projected)
                    pe.wait_ge(kst_ready, 1 + hd * 2 + hh)
                    for i in range(4):
                        last = pe.transpose(prep[0][0:2 * HD, i * P:(i + 1) * P],
                                            khl[:, b, 4 * hh + i, j].rearrange("p a r -> p (a r)").bitcast(F32), ident[:])
                    last.then_inc(k_turned, 1)
                    pe.wait_ge(qb_ready, 1 + hd * 2 + hh)
                    for i in range(4):
                        last = pe.transpose(prep[1][0:2 * HD, i * P:(i + 1) * P],
                                            qd[:, b, 4 * hh + i, j].rearrange("p a r -> p (a r)"), ident[:])
                    last.then_inc(q_turned, 1)

                def maximum(hd, r, x):
                    t, ck, w = CH[x]
                    pe.wait_ge(kst_ready, 1 + hd * 2 + (1 + t // 4))
                    pe.wait_ge(qb_ready, 1 + hd * 2 + (1 + t // 4))
                    if x < 2:
                        pe.wait_ge(mrow_ready, 1 + hd * 2)
                    else:
                        pe.wait_ge(max_taken, 1 + hd * NC + (x - 1))
                    out = mxp[x % 2]
                    q = slice(t * P, (t + 1) * P)
                    diagonal = ck == t // 4
                    full = max(w, FULL)
                    keys = kst[0:2 * HD, r, ck * W:ck * W + full]
                    pe.matmul(out[:, 0:full], qa[0:2 * HD, r, q], keys, start=True, stop=False)
                    last = pe.matmul(out[:, 0:full], qb[0:2 * HD, r, q], keys, start=False, stop=not diagonal)
                    if diagonal:
                        last = pe.matmul(out[:, w - P:w], ident_b[:], mask_qk[:], start=False, stop=True)
                    last.then_inc(max_ps, 1)

                def turn_maxima(hd, r):
                    pe.wait_ge(mcol_ready, hd + 1)
                    for hh in range(2):
                        for i in range(4):
                            last = pe.transpose(mxp[hh][0:2, i * P:(i + 1) * P],
                                                mcol[:, r, 4 * hh + i, :].bitcast(F32), ident[:])
                        last.then_inc(m_turned, 1)

                def score(hd, r, u):
                    c, kt, lo = ST[u]
                    if kt == 0:
                        pe.wait_ge(mrow_ready, 1 + hd * 2 + (c + 1))
                    pe.wait_ge(exp_done, 1 + hd * NS + (u - 1) if u else 1 + hd * NS)
                    left = min(lo, W - FULL)
                    q = slice(c * W + left, (c + 1) * W)
                    key = slice(kt * P, (kt + 1) * P)
                    out = sc[u % 2]
                    diagonal = kt >= 4 * c
                    pe.matmul(out[:, left:W], kst[:, r, key], qa[:, r, q], start=True, stop=False)
                    last = pe.matmul(out[:, left:W], kst[0:2 * HD, r, key], qb[0:2 * HD, r, q], start=False, stop=not diagonal)
                    if diagonal:
                        last = pe.matmul(out[:, lo:lo + P], ident_b[:], mask_kq[:], start=False, stop=True)
                    last.then_inc(score_ps, 1)

                def values(hd, j, b, u):
                    c, kt, lo = ST[u]
                    pe.wait_ge(exp_done, 1 + hd * NS + (u + 1))
                    if u == 0:
                        pe.wait_ge(o_taken, 1 + hd)
                    for i in range(lo // P, 4):
                        last = pe.matmul(acc[32 * i:32 * i + 32, c * P:(c + 1) * P], vst[:, b, kt, j, :],
                                         prob[:, u % PROBS, i * P:(i + 1) * P], start=(kt == 0), stop=(kt == 4 * c + i))
                    last.then_inc(av_done, 1)

                def turn_output(hd):
                    pe.wait_ge(o_taken, 1 + hd + 1)
                    pe.wait_ge(att_ready, 1 + hd)
                    for c in range(2):
                        last = pe.transpose(otr[:, c * P:(c + 1) * P], osb[:, c * P:(c + 1) * P], ident[:])
                    last.then_inc(o_turned, 1)

                def group(g, last):
                    for hd, half, j, b, events in slots(g, last):
                        ng, nb = next_half(g, b)
                        nj, tb = (j + 1, b) if j < J - 1 else (0, nb)
                        before = 0 if last and b == B - 1 else TILES[j][0]
                        for what, i in events:
                            if what == "S":
                                score(hd, j % 2, i)
                            elif what == "V":
                                values(hd, j, b, i)
                            elif what == "T":
                                if j == J - 1 and i == 0:
                                    pe.wait_ge(arr_ready, 1 + half * BT + 2 * BT)
                                turn(hd + 1, nj, tb, i, half * BT + (BT + before))
                            elif what == "X":
                                maximum(hd + 1, nj % 2, i)
                            elif what == "M":
                                turn_maxima(hd + 1, nj % 2)
                            elif what == "P":
                                project(ng, nb, half + 1, i, hd * 2 + 4)
                            else:
                                turn_output(hd)

                head_start(pe, k_turned, q_turned, av_done, o_turned)
                for t in range(BT):
                    project(0, 0, 0, t, None)
                pe.wait_ge(arr_ready, 1 + BT)
                for hh in range(2):
                    turn(0, 0, 0, hh, BT)
                for x in range(NC):
                    maximum(0, 0, x)
                turn_maxima(0, 0)
                with pe.Fori(0, G - 1) as g:
                    group(g, False)
                group(G - 1, True)

            @block.scalar
            def _(act):
                def take_raw(n, t):
                    act.wait_ge(proj_done, n * BT + (t + 1))
                    if not (isinstance(n, int) and n * BT + t < RAWS):
                        act.wait_ge(arr_ready, 1 + n * BT + (t + 1 - RAWS))
                    act.activation(raw[:, t % RAWS, :], prep[t % 2][:, 0:7 * J * CON], ACT.Copy).then_inc(raw_ready, 1)

                def operands(hd, r, hh):
                    cols = slice(hh * W, (hh + 1) * W)
                    act.wait_ge(k_turned, 1 + hd * 2 + (hh + 1))
                    if not (isinstance(hd, int) and hd < 2):
                        act.wait_ge(av_done, 1 + hd * NS - NS)
                    act.activation(kst[0:2 * HD, r, cols], prep[0][0:2 * HD, :], ACT.Copy).then_inc(kst_ready, 1)
                    act.wait_ge(q_turned, 1 + hd * 2 + (hh + 1))
                    act.activation(qa[0:2 * HD, r, cols], prep[1][0:2 * HD, :], ACT.Copy).then_inc(qa_ready, 1)

                def exponential(hd, u):
                    lo = ST[u][2]
                    act.wait_ge(score_ps, hd * NS + (u + 1))
                    if not (isinstance(hd, int) and hd * NS + u < PROBS):
                        act.wait_ge(av_done, 1 + hd * NS + (max(0, u + 1 - PROBS)))
                    act.activation(prob[:, u % PROBS, lo:W], sc[u % 2][:, lo:W], ACT.Exp, scale=SCALE).then_inc(exp_done, 1)

                def group(g, last):
                    for hd, half, j, b, events in slots(g, last):
                        for what, i in events:
                            if what == "S":
                                exponential(hd, i)
                            elif what == "T":
                                operands(hd + 1, (j + 1) % 2, i)
                            elif what == "P":
                                take_raw(half + 1, i)

                head_start(act, kst_ready, exp_done)
                for t in range(BT):
                    take_raw(0, t)
                for hh in range(2):
                    operands(0, 0, hh)
                with act.Fori(0, G - 1) as g:
                    group(g, False)
                group(G - 1, True)

            @block.gpsimd
            def _(pool):
                def arrange(n, b):
                    PSTEP = 2 * BT
                    if not (isinstance(n, int) and n < 2):
                        pool.wait_ge(k_turned, 1 + n * (2 * J) - 2 * J)
                        pool.wait_ge(q_turned, 1 + n * (2 * J) - 2 * J)
                        pool.wait_ge(av_done, 1 + n * (NS * J) - NS * J)
                    for t in range(BT):
                        u, w = t % 2, t % RAWS
                        pool.wait_ge(raw_ready, n * BT + (t + 1))
                        rope = raw[:, w, 0:2 * J * ROPE].rearrange("p (h r) -> p h r", r=ROPE)
                        cos = k["cos"][:, t:t + 1, :].to_broadcast([P, 2 * J, ROPE])
                        pool.tensor_tensor(roc[:, u], rope, cos, ALU.mult)
                        for lo, hi in ((0, ROPE // 2), (ROPE // 2, 0)):
                            sin = k["sin"][:, t:t + 1, lo:lo + ROPE // 2].to_broadcast([P, 2 * J, ROPE // 2])
                            pool.tensor_tensor(ros[:, u, :, lo:lo + ROPE // 2], rope[:, :, hi:hi + ROPE // 2], sin, ALU.mult)
                        q0, k0, v0 = 2 * J * ROPE, 2 * J * ROPE + J * CON, 2 * J * ROPE + 2 * J * CON
                        for r in range(2):
                            pool.tensor_copy(qd[:, b, t, :, r, 0:CON], raw[:, w, q0:k0].rearrange("p (h r) -> p h r", r=CON))
                        keys = raw[:, w, k0:v0].rearrange("p (h r) -> p h r", r=CON)
                        pool.tensor_copy(kraw[:, u, :, 0:CON], keys)
                        pool.tensor_copy(khl[:, b, t, :, 0, 0:CON], keys)
                        pool.tensor_copy(vst[:, b, t, :, 0:CON],
                                         raw[:, w, v0:].rearrange("p (h r) -> p h r", r=CON)).then_inc(pool_step, 1)
                        pool.wait_ge(pool_step, n * PSTEP + (2 * t + 1))
                        for r in range(2):
                            pool.tensor_tensor(qd[:, b, t, :, r, CON:HD], roc[:, u, J:2 * J], ros[:, u, J:2 * J], ALU.add)
                        pool.tensor_tensor(kraw[:, u, :, CON:HD], roc[:, u, 0:J], ros[:, u, 0:J], ALU.add)
                        pool.tensor_tensor(khl[:, b, t, :, 0, CON:HD], roc[:, u, 0:J], ros[:, u, 0:J],
                                           ALU.add).then_inc(pool_step, 1)
                        pool.wait_ge(pool_step, n * PSTEP + (2 * t + 2))
                        pool.tensor_tensor(khl[:, b, t, :, 1, :], kraw[:, u], khl[:, b, t, :, 0, :].bitcast(F32),
                                           ALU.subtract).then_inc(arr_ready, 1)

                head_start(pool, arr_ready)
                arrange(0, 0)
                with pool.Fori(0, G - 1) as g:
                    arrange(g * 2 + 1, 1)
                    arrange(g * 2 + 2, 0)
                arrange(2 * G - 1, 1)

            @block.vector
            def _(dve):
                def low_queries(hd, r, hh):
                    cols = slice(hh * W, (hh + 1) * W)
                    dve.wait_ge(qa_ready, hd * 2 + (hh + 1))
                    dve.tensor_tensor(qb[0:2 * HD, r, cols], prep[1][0:2 * HD, :],
                                      qa[0:2 * HD, r, cols].bitcast(F32), ALU.subtract).then_inc(qb_ready, 1)

                def maximum(hd, x):
                    t, ck, w = CH[x]
                    dve.wait_ge(max_ps, hd * NC + (x + 1))
                    dve.tensor_reduce(k["pmax"][:, ck, t:t + 1], mxp[x % 2][:, 0:w], AX.X, ALU.max).then_inc(max_taken, 1)

                def maxima(hd, r):
                    dve.wait_ge(max_taken, 1 + hd * NC + NC)
                    dve.tensor_tensor(mx[:, r], k["pmax"][:, 0, :], k["pmax"][:, 1, :], ALU.max).then_inc(dve_step, 1)
                    dve.wait_ge(dve_step, hd * 2 + 1)
                    dve.tensor_scalar(mcol[:, r, :, 0], mx[:, r], -1.0, None, ALU.mult).then_inc(dve_step, 1)
                    dve.wait_ge(dve_step, hd * 2 + 2)
                    dve.scalar_tensor_tensor(out=mcol[:, r, :, 1], in0=mx[:, r], scalar=-1.0,
                                             in1=mcol[:, r, :, 0].bitcast(F32), op0=ALU.mult, op1=ALU.subtract).then_inc(mcol_ready, 1)

                def max_rows(hd, r):
                    for hh in range(2):
                        dve.wait_ge(m_turned, hd * 2 + (hh + 1))
                        dve.tensor_copy(qa[2 * HD:2 * HD + 2, r, hh * W:(hh + 1) * W], mxp[hh][0:2, :]).then_inc(mrow_ready, 1)

                def group(g, last):
                    for hd, half, j, b, events in slots(g, last):
                        for what, i in events:
                            if what == "T":
                                low_queries(hd + 1, (j + 1) % 2, i)
                            elif what == "X":
                                maximum(hd + 1, i)
                            elif what == "M":
                                maxima(hd + 1, (j + 1) % 2)
                        dve.wait_ge(av_done, 1 + hd * NS + NS)
                        dve.wait_ge(o_turned, 1 + hd)
                        dve.tensor_copy(osb[:], acc[:, 0:2 * P]).then_inc(o_taken, 1)
                        if ("M", 0) in events:
                            max_rows(hd + 1, (j + 1) % 2)
                        dve.wait_ge(o_turned, 1 + hd + 1)
                        o = otr[:, 0:2 * P].rearrange("p (t r) -> p t r", t=BT)
                        dve.wait_ge(att_ready, 1 + hd)
                        dve.reciprocal(rcp[:], o[:, :, CON]).then_inc(o_step, 1)
                        dve.wait_ge(o_step, hd + 1)
                        dst = att[:, b * BT:(b + 1) * BT, bass.ds((g * J + j) * CON, CON)]
                        dve.tensor_tensor(dst, o[:, :, 0:CON],
                                          rcp[:].rearrange("p (t a) -> p t a", a=1).to_broadcast([P, BT, CON]),
                                          ALU.mult).then_inc(att_ready, 1)

                head_start(dve, qb_ready, max_taken, mrow_ready, o_taken, att_ready)
                for hh in range(2):
                    low_queries(0, 0, hh)
                for x in range(NC):
                    maximum(0, x)
                maxima(0, 0)
                max_rows(0, 0)
                with dve.Fori(0, G - 1) as g:
                    group(g, False)
                group(G - 1, True)


def experts(nc, d, k):
    with ExitStack() as ctx:
        def sb(name, shape, dt=F32):
            return ctx.enter_context(nc.sbuf_tensor(name, shape, dt))

        def sem(name):
            return ctx.enter_context(nc.semaphore(name))

        att, h, ident = k["att"], k["h"], k["ident"]
        wo = sb("wo", [P, DC, D])
        attT = sb("attT", [P, DC, B * T])
        stats = sb("stats2", [P, TT, 6])
        mv = sb("mv2", [P, TT, 2])
        ve = sb("ve2", [P, TT])
        sd = sb("sd2", [P, TT])
        rstd = sb("rstd2", [P, TT])
        xn = att
        yT = attT
        yh = sb("yh", [P, DC, B * T], F32R)
        yl = sb("yl", [P, DC, B * T], F32R)
        gw = sb("gw", [P, DC, E])
        gu = sb("gu", [P, 2, DC, 2 * F])
        dn = sb("dn", [P, 2, FC, D])
        guh = sb("guh", [P, 2, DC, 2 * F], F32R)
        gul = sb("gul", [P, 2, DC, 2 * F], F32R)
        dnh = sb("dnh", [P, 2, FC, D], F32R)
        dnl = sb("dnl", [P, 2, FC, D], F32R)
        sg = sb("sg", [P, 2, FC, W])
        hm = sb("hm", [P, 2, FC, W])
        hmh = sb("hmh", [P, 2, FC, W], F32R)
        hml = sb("hml", [P, 2, FC, W], F32R)
        R = {n: sb("r_" + n, [P, TT, E]) for n in ("lg", "ex", "p", "eq", "cd", "f1", "f2", "p2", "wd", "cb")}
        S = {n: sb("s_" + n, [P, TT]) for n in ("mx", "sum", "r", "m1", "m2", "c", "w1", "w2", "t")}
        rank = sb("rank", [P, E])
        M = {n: sb("m_" + n, [P, E, E]) for n in ("sim", "ms", "eq", "cd", "map", "id", "t")}
        V = {n: sb("v_" + n, [P, E]) for n in ("pres", "prim", "neg", "bs", "c", "go", "stay")}
        prod = sb("prod", [P, TT, E, E])
        ones = sb("ones", [P, P])
        iot = sb("iot", [P, E])

        ps = [ctx.enter_context(nc.psum_tensor(f"pc{i}", [P, W], F32)) for i in range(8)]

        (wo_in, gw_in, at_turned, at_ready, o_ps, h_ready, var_ready, sd_ready, xn_ready, y_turned, y_full, y_hi, y_lo,
         lg_ps, lg_max, ex_ready, pres_ready, pres_ps, cb_ready, w_split, gu_ps, sg_ready, hm_ready,
         hmh_ready, hml_ready, w_hi, dn_ps, acc_done, dve_step, pool_step, out_done, const2) = (sem(n) for n in (
             "wo_in", "gw_in", "at_turned", "at_ready", "o_ps", "h_ready", "var2_ready", "sd2_ready", "xn2_ready",
             "y_turned", "y_full", "y_hi", "y_lo", "lg_ps", "lg_max", "ex2_ready", "pres_ready", "pres_ps", "cb_ready",
             "w_split", "gu_ps", "sg_ready", "hm_ready", "hmh_ready", "hml_ready", "w_hi", "dn_ps",
             "acc_done", "dve2_step", "pool2_step", "out_done", "const2"))

        ex_in = [sem(f"ex_in{u}") for u in range(2)]

        with nc.Block() as block:
            @block.sync
            def _(sp):
                sp.dma_start(wo[:], d["W_o"].rearrange("(c p) n -> p c n", p=P)).then_inc(wo_in, 16)
                sp.dma_start(gw[:], d["gateT"].rearrange("(c p) e -> p c e", p=P)).then_inc(gw_in, 16)
                sp.dma_start(M["sim"][:].rearrange("p a b -> p (a b)"),
                             d["sim"].rearrange("a b -> (a b)").rearrange("(o n) -> o n", o=1).to_broadcast([P, E * E])).then_inc(gw_in, 16)
                with sp.Fori(0, E // 2) as e2:
                    for u in range(2):
                        e = e2 * 2 + u
                        sp.wait_ge(w_split, 1 + e2 * 2 if u == 0 else e2 * 2)
                        sp.dma_start(gu[:, u], d["guT"][bass.ds(e, 1)].rearrange("o (c p) f -> p (o c) f", p=P)).then_inc(ex_in[u], 16)
                        sp.dma_start(dn[:, u], d["dnT"][bass.ds(e, 1)].rearrange("o (c p) f -> p (o c) f", p=P)).then_inc(ex_in[u], 16)
                sp.wait_ge(acc_done, 1 + E * NW)
                sp.dma_start(d["out"].rearrange("(t p) e -> p t e", p=P), h[:]).then_inc(out_done, 16)
                sp.wait_ge(out_done, 16)

            @block.gpsimd
            def _(pool):
                pool.iota(iot[:], pattern=[[-1, E]], base=E, channel_multiplier=0,
                          allow_small_or_imprecise_dtypes=True).then_inc(pool_step, 1)
                pool.memset(M["id"][:], 0.0).then_inc(pool_step, 1)
                pool.wait_ge(pool_step, 2)
                pool.affine_select(out=M["id"][:], in_=M["id"][:], compare_op=ALU.not_equal, fill=1.0,
                                   base=0, pattern=[[1, E], [-1, E]], channel_multiplier=0).then_inc(const2, 1)
                pool.memset(ones[:], 1.0).then_inc(const2, 1)
                head_start(pool, w_split)
                with pool.Fori(0, E // 2) as e2:
                    for u in range(2):
                        e = e2 * 2 + u
                        pool.wait_ge(w_hi, e + 1)
                        pool.tensor_tensor(gul[:, u], gu[:, u], guh[:, u].bitcast(F32), ALU.subtract)
                        pool.tensor_tensor(dnl[:, u], dn[:, u], dnh[:, u].bitcast(F32), ALU.subtract).then_inc(w_split, 1)

            @block.tensor
            def _(pe):
                for n in range(NW):
                    for c in range(DC):
                        m = n * DC + c
                        if m >= 4:
                            pe.wait_ge(at_ready, m - 3)
                        for i in range(4):
                            last = pe.transpose(ps[m % 4][:, i * P:(i + 1) * P], att[:, 4 * n + i, c * P:(c + 1) * P], ident[:])
                        last.then_inc(at_turned, 1)
                pe.wait_ge(wo_in, 16)
                for t in range(TT):
                    pe.wait_ge(at_ready, (t // 4) * DC + 2)
                    if t >= 4:
                        pe.wait_ge(h_ready, t - 3)
                    for c in range(DC):
                        last = pe.matmul(ps[4 + t % 4][:, 0:D], attT[:, c, t * P:(t + 1) * P], wo[:, c, :], start=(c == 0), stop=(c == DC - 1))
                    last.then_inc(o_ps, 1)
                for n in range(NW):
                    pe.wait_ge(xn_ready, 4 * n + 4)
                    for c in range(DC):
                        m = n * DC + c
                        if m >= 4:
                            pe.wait_ge(y_lo, m - 3)
                        for i in range(4):
                            last = pe.transpose(ps[m % 4][:, i * P:(i + 1) * P], xn[:, 4 * n + i, c * P:(c + 1) * P], ident[:])
                        last.then_inc(y_turned, 1)
                pe.wait_ge(gw_in, 32)
                pe.wait_ge(y_full, NW * DC)
                for t in range(TT):
                    for c in range(DC):
                        last = pe.matmul(ps[4][:, t * E:(t + 1) * E], yT[:, c, t * P:(t + 1) * P], gw[:, c, :], start=(c == 0), stop=(c == DC - 1))
                last.then_inc(lg_ps, 1)
                pe.wait_ge(pres_ready, 1)
                pe.wait_ge(const2, 2)
                pe.matmul(ps[5][:, 0:E], ones[:], V["pres"][:], start=True, stop=True).then_inc(pres_ps, 1)
                pe.wait_ge(cb_ready, 1)
                pe.wait_ge(y_lo, NW * DC)

                def up(e2, u, n):
                    it = e2 * (2 * NW) + u * NW + n
                    cols = slice(n * W, (n + 1) * W)
                    pe.wait_ge(w_split, 1 + e2 * 2 + u + 1)
                    for fc in range(FC):
                        pe.wait_ge(hm_ready, 1 + it * FC if fc == 0 else it * FC)
                        for s in range(2):
                            f = slice(s * F + fc * P, s * F + (fc + 1) * P)
                            for c in range(DC):
                                last = three(pe, ps[2 * fc + s][:], (guh[:, u, c, f], gul[:, u, c, f]),
                                             (yh[:, c, cols], yl[:, c, cols]), c == 0, c == DC - 1)
                        last.then_inc(gu_ps, 1)

                def down(e2, u, n):
                    it = e2 * (2 * NW) + u * NW + n
                    r = n % 2
                    pe.wait_ge(hml_ready, it * FC + FC)
                    for i in range(4):
                        pe.wait_ge(acc_done, 1 + it)
                        tok = slice(i * P, (i + 1) * P)
                        for fc in range(FC):
                            last = three(pe, ps[4 + i][:, 0:D], (hmh[:, r, fc, tok], hml[:, r, fc, tok]),
                                         (dnh[:, u, fc, :], dnl[:, u, fc, :]), fc == 0, fc == FC - 1)
                        last.then_inc(dn_ps, 1)

                head_start(pe, dn_ps)
                with pe.Fori(0, E // 2) as e2:
                    for u in range(2):
                        for n in range(NW):
                            up(e2, u, n)
                            down(e2, u, n)

            @block.scalar
            def _(act):
                def high_weights(e2, u):
                    act.wait_ge(ex_in[u], e2 * 32 + 32)
                    act.wait_ge(dn_ps, 1 + e2 * (2 * 4 * NW))
                    act.activation(guh[:, u], gu[:, u], ACT.Copy)
                    act.activation(dnh[:, u], dn[:, u], ACT.Copy).then_inc(w_hi, 1)

                for n in range(NW):
                    for c in range(DC):
                        m = n * DC + c
                        act.wait_ge(at_turned, m + 1)
                        act.activation(attT[:, c, n * W:(n + 1) * W], ps[m % 4][:], ACT.Copy).then_inc(at_ready, 1)
                act.wait_ge(var_ready, 1)
                act.activation(sd[:], ve[:], ACT.Sqrt).then_inc(sd_ready, 1)
                act.wait_ge(o_ps, TT)
                for n in range(NW):
                    for c in range(DC):
                        m = n * DC + c
                        cols = slice(n * W, (n + 1) * W)
                        act.wait_ge(y_turned, m + 1)
                        act.activation(yT[:, c, cols], ps[m % 4][:], ACT.Copy).then_inc(y_full, 1)
                        act.activation(yh[:, c, cols], ps[m % 4][:], ACT.Copy).then_inc(y_hi, 1)
                act.wait_ge(lg_max, 1)
                act.activation(R["ex"][:], R["lg"][:], ACT.Exp).then_inc(ex_ready, 1)
                with act.Fori(0, E // 2) as e2:
                    high_weights(e2, 0)
                    high_weights(e2, 1)
                    for u in range(2):
                        for n in range(NW):
                            it = e2 * (2 * NW) + u * NW + n
                            r = n % 2
                            for fc in range(FC):
                                act.wait_ge(gu_ps, it * FC + fc + 1)
                                act.activation(sg[:, r, fc, :], ps[2 * fc][:], ACT.Silu).then_inc(sg_ready, 1)
                            for fc in range(FC):
                                act.wait_ge(hm_ready, 1 + it * FC + fc + 1)
                                act.activation(hmh[:, r, fc, :], hm[:, r, fc, :], ACT.Copy).then_inc(hmh_ready, 1)

            @block.vector
            def _(dve):
                step = Chain(dve, dve_step)

                def did(ins):
                    step.did(ins)
                    step.settle()

                for t in range(TT):
                    dve.wait_ge(o_ps, t + 1)
                    dve.tensor_tensor(h[:, t, :], h[:, t, :], ps[4 + t % 4][:, 0:D], ALU.add).then_inc(h_ready, 1)
                dve.wait_ge(h_ready, TT)
                for t in range(TT):
                    step.did(dve.bn_stats(stats[:, t, :], h[:, t, :]))
                step.settle()
                for t in range(TT):
                    step.did(dve.bn_aggr(mv[:, t, :], stats[:, t, :]))
                step.settle()
                dve.tensor_scalar(ve[:], mv[:, :, 1], 1e-5, None, ALU.add).then_inc(var_ready, 1)
                dve.wait_ge(sd_ready, 1)
                did(dve.reciprocal(rstd[:], sd[:]))
                dve.wait_ge(at_turned, NW * DC)
                for t in range(TT):
                    dve.tensor_scalar(xn[:, t, :], h[:, t, :], mv[:, t, 0:1], rstd[:, t:t + 1],
                                      ALU.subtract, ALU.mult).then_inc(xn_ready, 1)
                for n in range(NW):
                    for c in range(DC):
                        m = n * DC + c
                        cols = slice(n * W, (n + 1) * W)
                        dve.wait_ge(y_hi, m + 1)
                        dve.tensor_tensor(yl[:, c, cols], ps[m % 4][:], yh[:, c, cols].bitcast(F32), ALU.subtract).then_inc(y_lo, 1)

                def wide(s):
                    return S[s][:].rearrange("p (t a) -> p t a", a=1).to_broadcast([P, TT, E])

                def each(v):
                    return v[:].rearrange("p (a e) -> p a e", a=1).to_broadcast([P, TT, E])

                dve.wait_ge(lg_ps, 1)
                lg = ps[4][:, 0:TT * E].rearrange("p (t e) -> p t e", e=E)
                did(dve.tensor_reduce(S["mx"][:], lg, AX.X, ALU.max))
                dve.tensor_tensor(R["lg"][:], lg, wide("mx"), ALU.subtract).then_inc(lg_max, 1)
                dve.wait_ge(ex_ready, 1)
                did(dve.tensor_reduce(S["sum"][:], R["ex"][:], AX.X, ALU.add))
                did(dve.reciprocal(S["r"][:], S["sum"][:]))
                did(dve.tensor_tensor(R["p"][:], R["ex"][:], wide("r"), ALU.mult))
                dve.wait_ge(const2, 2)

                def largest(src, m, f):
                    did(dve.tensor_reduce(S[m][:], R[src][:], AX.X, ALU.max))
                    did(dve.tensor_tensor(R["eq"][:], R[src][:], wide(m), ALU.is_equal))
                    did(dve.tensor_tensor(R["cd"][:], R["eq"][:], each(iot), ALU.mult))
                    did(dve.tensor_reduce(S["c"][:], R["cd"][:], AX.X, ALU.max))
                    did(dve.tensor_tensor(R[f][:], each(iot), wide("c"), ALU.is_equal))

                largest("p", "m1", "f1")
                did(dve.scalar_tensor_tensor(out=R["p2"][:], in0=R["f1"][:], scalar=-2.0, in1=R["p"][:], op0=ALU.mult, op1=ALU.add))
                dve.tensor_reduce(V["pres"][:], R["f1"][:].rearrange("p t e -> p e t"), AX.X, ALU.add).then_inc(pres_ready, 1)
                largest("p2", "m2", "f2")
                did(dve.tensor_tensor(S["t"][:], S["m1"][:], S["m2"][:], ALU.add))
                did(dve.tensor_scalar(S["t"][:], S["t"][:], 1e-12, None, ALU.max))
                did(dve.reciprocal(S["r"][:], S["t"][:]))
                did(dve.tensor_tensor(S["w1"][:], S["m1"][:], S["r"][:], ALU.mult))
                did(dve.tensor_tensor(S["w2"][:], S["m2"][:], S["r"][:], ALU.mult))
                did(dve.tensor_tensor(R["wd"][:], R["f1"][:], wide("w1"), ALU.mult))
                did(dve.tensor_tensor(R["cd"][:], R["f2"][:], wide("w2"), ALU.mult))
                did(dve.tensor_tensor(R["wd"][:], R["wd"][:], R["cd"][:], ALU.add))
                def over_i(v):
                    return v[:].rearrange("p (a e) -> p a e", a=1).to_broadcast([P, E, E])

                def over_j(v):
                    return v[:].rearrange("p (e a) -> p e a", a=1).to_broadcast([P, E, E])

                dve.wait_ge(pres_ps, 1)
                dve.wait_ge(gw_in, 32)
                did(dve.tensor_scalar(V["prim"][:], ps[5][:, 0:E], 0.5, None, ALU.is_ge))
                did(dve.tensor_scalar(V["neg"][:], V["prim"][:], -LOWEST, LOWEST, ALU.mult, ALU.add))
                did(dve.tensor_tensor(M["ms"][:], M["sim"][:], over_i(V["prim"]), ALU.mult))
                did(dve.tensor_tensor(M["ms"][:], M["ms"][:], over_i(V["neg"]), ALU.add))
                did(dve.tensor_reduce(V["bs"][:], M["ms"][:], AX.X, ALU.max))
                did(dve.tensor_tensor(M["eq"][:], M["ms"][:], over_j(V["bs"]), ALU.is_equal))
                did(dve.tensor_tensor(M["cd"][:], M["eq"][:], over_i(iot), ALU.mult))
                did(dve.tensor_reduce(V["c"][:], M["cd"][:], AX.X, ALU.max))
                did(dve.tensor_tensor(M["map"][:], over_i(iot), over_j(V["c"]), ALU.is_equal))
                did(dve.tensor_scalar(V["go"][:], V["bs"][:], 0.7, None, ALU.is_ge))
                did(dve.tensor_tensor(V["go"][:], V["go"][:], V["prim"][:], ALU.is_gt))
                did(dve.tensor_scalar(V["stay"][:], V["go"][:], -1.0, 1.0, ALU.mult, ALU.add))
                did(dve.tensor_tensor(M["map"][:], M["map"][:], over_j(V["go"]), ALU.mult))
                did(dve.tensor_tensor(M["t"][:], M["id"][:], over_j(V["stay"]), ALU.mult))
                did(dve.tensor_tensor(M["map"][:], M["map"][:], M["t"][:], ALU.add))
                for j in range(E):
                    step.did(dve.tensor_tensor(prod[:, :, j, :], R["wd"][:], M["map"][:, :, j].rearrange("p (a e) -> p a e", a=1).to_broadcast([P, TT, E]), ALU.mult))
                step.settle()
                dve.tensor_reduce(R["cb"][:], prod[:], AX.X, ALU.add).then_inc(cb_ready, 1)
                dve.wait_ge(cb_ready, 1)

                head_start(dve, hm_ready, acc_done)
                with dve.Fori(0, E // 2) as e2:
                    for u in range(2):
                        for n in range(NW):
                            it = e2 * (2 * NW) + u * NW + n
                            r = n % 2
                            for fc in range(FC):
                                dve.wait_ge(sg_ready, it * FC + fc + 1)
                                dve.tensor_tensor(hm[:, r, fc, :], sg[:, r, fc, :], ps[2 * fc + 1][:], ALU.mult).then_inc(hm_ready, 1)
                            for fc in range(FC):
                                dve.wait_ge(hmh_ready, it * FC + fc + 1)
                                dve.tensor_tensor(hml[:, r, fc, :], hm[:, r, fc, :], hmh[:, r, fc, :].bitcast(F32), ALU.subtract).then_inc(hml_ready, 1)
                            for i in range(4):
                                t = 4 * n + i
                                dve.wait_ge(dn_ps, 1 + it * 4 + i + 1)
                                last = dve.scalar_tensor_tensor(out=h[:, t, :], in0=ps[4 + i][:, 0:D],
                                                                scalar=R["cb"][:, t, bass.ds(e2 * 2 + u, 1)], in1=h[:, t, :],
                                                                op0=ALU.mult, op1=ALU.add)
                            last.then_inc(acc_done, 1)


def tower(nc, d):
    with ExitStack() as ctx:
        def sb(name, shape, dt=F32):
            return ctx.enter_context(nc.sbuf_tensor(name, shape, dt))

        k = {
            "h": sb("h", [P, TT, D]),
            "cos": sb("cos", [P, BT, ROPE]), "sin": sb("sin", [P, BT, ROPE]),
            "ident": sb("ident", [P, P]), "ident_b": sb("ident_b", [P, P], BF16),
            "mask_qk": sb("mask_qk", [P, P], BF16), "mask_kq": sb("mask_kq", [P, P], BF16),
            "pmax": sb("pmax", [P, 2, BT]),
        }
        with ExitStack() as inner:
            def sbi(name, shape, dt=F32):
                return inner.enter_context(nc.sbuf_tensor(name, shape, dt))

            att = sb("att", [P, TT, D])
            k.update({
                "xn": sbi("xnT", [P, DC, B * T]), "qc": sbi("qc", [P, B * T]), "kv": sbi("kv", [P, B * T], F32R),
                "wkr": sbi("wkr", [P, DC, HEADS * ROPE]), "wqx": sbi("wqx", [P, G, J * HD]),
                "wkx": sbi("wkx", [P, G, 2 * J * CON]),
                "vst": sbi("vst", [P, 2, BT, J, 32]),
                "kst": sbi("kst", [2 * HD + 2, 2, T], F32R),
                "att": att,
            })
            k["ones_rows"] = k["kst"][2 * HD:2 * HD + 2, :, :]
            prepare(nc, d, k)
            k["qa"] = sbi("qa", [2 * HD + 2, 2, T], F32R)
            k["qb"] = sbi("qb", [2 * HD, 2, T], F32R)
            attention(nc, k)
        experts(nc, d, k)


_WEIGHTS = ['L0_tok_W1', 'L0_tok_b1', 'L0_tok_W2', 'L0_tok_b2', 'L0_attn_W_kv', 'L0_attn_g_kv', 'L0_attn_W_kdec',
            'L0_attn_W_vdec', 'L0_attn_W_q', 'L0_attn_W_qdec', 'L0_attn_W_krope', 'L0_attn_W_qrope', 'L0_attn_W_o']


def kernel(**inputs):
    import numpy as np
    import concourse.bacc as bacc
    from concourse.bass_utils import run_bass_kernel_spmd

    nc = bacc.Bacc("TRN2", target_bir_lowering=False, num_devices=1, dynamic_dma_scratch_size=1024)
    nc.disable_value_cache = True
    x = np.asarray(inputs["x"])
    tokens = x.reshape(B * T, D)
    arrays = {n.split("_", 2)[2]: np.ascontiguousarray(inputs[n]) for n in _WEIGHTS}
    arrays["x"] = np.ascontiguousarray(tokens)
    arrays["xT"] = np.ascontiguousarray(tokens.T)
    arrays["gateT"] = np.ascontiguousarray(np.asarray(inputs["L0_ffn_gate_weight"]).T)
    arrays["guT"] = np.ascontiguousarray(np.asarray(inputs["L0_ffn_gate_up_proj"]).transpose(0, 2, 1))
    arrays["dnT"] = np.ascontiguousarray(np.asarray(inputs["L0_ffn_down_proj"]).transpose(0, 2, 1))
    arrays["sim"] = np.ascontiguousarray(inputs["L0_ffn_similarity_matrix"])
    inv_freq = 1.0 / 10000.0 ** (np.arange(0, ROPE, 2, dtype=np.float32) / ROPE)
    freqs = np.outer(np.arange(T, dtype=np.float32), inv_freq)
    arrays["cos"] = np.cos(np.concatenate([freqs, freqs], -1)).astype(np.float32)
    arrays["sin"] = np.sin(np.concatenate([-freqs, freqs], -1)).astype(np.float32)

    d = {n: nc.dram_tensor("in_" + n, a.shape, mybir.dt.from_np(a.dtype), kind="ExternalInput").ap()
         for n, a in arrays.items()}
    d["out"] = nc.dram_tensor("out_h", (B * T, D), F32, kind="ExternalOutput").ap()
    tower(nc, d)
    r = run_bass_kernel_spmd(nc, [{"in_" + n: a for n, a in arrays.items()}], core_ids=[0])
    return r.results[0]["out_h"].reshape(B, T, D)
```

```python
from contextlib import ExitStack

import concourse.bass as bass
from concourse import mybir

F32 = mybir.dt.float32
F32R = mybir.dt.float32r
BF16 = mybir.dt.bfloat16
ALU = mybir.AluOpType
ACT = mybir.ActivationFunctionType
AX = mybir.AxisListType

P = 128
B, T, D = 2, 1024, 256
TT = B * T // P
BT = T // P
DC = D // P
HEADS, CON, ROPE = 16, 16, 32
HD = CON + ROPE
J = 4
G = HEADS // J
KVR, QR = 64, 128
E, F = 8, 256
FC = F // P
LOW = 64
ROWS = LOW + HD
TOKH = 128
W = 512
FULL = 256
NW = B * T // W
BIG = float(2 ** 100)
LOWEST = -3.0e38


class Chain:

    def __init__(self, eng, sem, base=0):
        self.eng, self.sem, self.base, self.n = eng, sem, base, 0

    def did(self, ins):
        self.n += 1
        ins.then_inc(self.sem, 1)
        return ins

    def settle(self):
        self.eng.wait_ge(self.sem, self.base + self.n)


def head_start(eng, *sems):
    for s in sems:
        eng.sem_inc(s, 1)


def three(pe, out, stat, mov, first=True, last=True):
    (sh, sl), (mh, ml) = stat, mov
    pe.matmul(out, sh, mh, start=first, stop=False)
    pe.matmul(out, sh, ml, start=False, stop=False)
    return pe.matmul(out, sl, mh, start=False, stop=last)


POOL_WEIGHTS = 2
PREPARE = [(stage, int(n)) for stage, n in (event.split(":") for event in """
    sums:0 sums:1 norm:0 sums:2 norm:1 turn:0 sums:3 norm:2 turn:1 norm:3 rank:0 turn:2
    rank:1 rms:0 turn:3 rank:2 rms:1 stack:0 rank:3 rms:2 stack:1 rms:3 stack:2 stack:3""".split())]


def prepare(nc, d, k):
    with ExitStack() as ctx:
        def sb(name, shape, dt=F32):
            return ctx.enter_context(nc.sbuf_tensor(name, shape, dt))

        def sem(name):
            return ctx.enter_context(nc.semaphore(name))

        xT = sb("xT", [P, DC, B * T])
        xin = sb("xin", [P, TT, D])
        w1 = sb("w1", [P, DC, TOKH])
        w2 = sb("w2", [P, 1])
        b1 = sb("b1", [P, 1])
        b2 = sb("b2", [P, 1])
        hid = sb("hid", [P, 2, W])
        en = sb("en", [P, TT])
        de = sb("de", [P, TT])
        ex = sb("ex", [P, TT])
        rs = sb("rs", [P, TT])
        wt = sb("wt", [P, TT])
        stats = sb("stats", [P, TT, 6])
        mv = sb("mv", [P, TT, 2])
        ve = sb("ve", [P, TT])
        sd = sb("sd", [P, TT])
        rstd = sb("rstd", [P, TT])
        xn = xin
        wq = sb("wq", [P, DC, QR])
        wkv = sb("wkv", [P, DC, KVR])
        gkv = sb("gkv", [P, KVR])
        kvsq = sb("kvsq", [P, TT, KVR])
        kvn = sb("kvn", [P, TT, KVR])
        kvd = sb("kvd", [P, TT, 2 * KVR])
        kvm = sb("kvm", [P, TT])
        kvs = sb("kvs", [P, TT])
        kvr = sb("kvr", [P, TT])
        kvhi = sb("kvhi", [P, 2, W], F32R)
        wkr, wqx, wkx = k["wkr"], k["wqx"], k["wkx"]
        lowrow = sb("lowrow", [P, 1])
        mask1 = sb("mask1", [P, P])
        mask2 = sb("mask2", [P, P])

        ps = [ctx.enter_context(nc.psum_tensor(f"pa{i}", [P, W], F32)) for i in range(8)]

        xT_in, x_in = ([sem(f"{name}{n}") for n in range(NW)] for name in ("xT_in", "x_in"))
        tok_w_in, low_w_in, dec_w_in, tab_in = (sem(n) for n in (
            "tok_w_in", "low_w_in", "dec_w_in", "tab_in"))
        hid_ps, hid_ready, en_ps = sem("hid_ps"), sem("hid_ready"), sem("en_ps")
        diff_ready, exp_ready, var_ready, sd_ready = (sem(n) for n in ("diff_ready", "exp_ready", "var_ready", "sd_ready"))
        xn_ready, turned, xn_turned = (sem(n) for n in ("xn_ready", "turned", "xn_turned"))
        const_ready, kv_ps, kv_sq, kv_mean, kv_sd = (sem(n) for n in (
            "const_ready", "kv_ps", "kv_sq", "kv_mean", "kv_sd"))
        qc_ps, qc_ready = sem("qc_ps"), sem("qc_ready")
        kvn_ready, kv_turned, kv_hi, kv_split = sem("kvn_ready"), sem("kv_turned"), sem("kv_hi"), sem("kv_split")
        dve_step, pool_step = sem("dve_step"), sem("pool_step")
        wt_ready, h_weighted, kvn_read = sem("wt_ready"), sem("h_weighted"), sem("kvn_read")

        with nc.Block() as block:
            @block.sync
            def _(sp):
                sp.dma_start(w1[:], d["W1"].rearrange("(c p) h -> p c h", p=P)).then_inc(tok_w_in, 16)
                for n in range(NW):
                    sp.dma_start(xT[:, :, n * W:(n + 1) * W],
                                 d["xT"].rearrange("(c p) n -> p c n", p=P)[:, :, n * W:(n + 1) * W]).then_inc(xT_in[n], 16)
                    if n == 0:
                        sp.dma_start(b1[:], d["b1"].rearrange("(p a) -> p a", a=1)).then_inc(tok_w_in, 16)
                        sp.dma_start(w2[:], d["W2"]).then_inc(tok_w_in, 16)
                        sp.dma_start(b2[:], d["b2"].rearrange("(p a) -> p a", a=1).to_broadcast([P, 1])).then_inc(tok_w_in, 16)
                for n in range(NW):
                    sp.dma_start(xin[:, 4 * n:4 * n + 4, :],
                                 d["x"].rearrange("(t p) e -> p t e", p=P)[:, 4 * n:4 * n + 4, :]).then_inc(x_in[n], 16)
                sp.dma_start(wq[:], d["W_q"].rearrange("(c p) r -> p c r", p=P)).then_inc(low_w_in, 16)
                sp.dma_start(wkv[:], d["W_kv"].rearrange("(c p) r -> p c r", p=P)).then_inc(low_w_in, 16)
                sp.dma_start(gkv[:], d["g_kv"].rearrange("(a r) -> a r", a=1).to_broadcast([P, KVR])).then_inc(low_w_in, 16)
                sp.dma_start(wkr[:], d["W_krope"].rearrange("(c p) n -> p c n", p=P)).then_inc(dec_w_in, 16)
                sp.dma_start(wqx[:, :, 0:J * ROPE], d["W_qrope"].rearrange("p (g n) -> p g n", g=G)).then_inc(dec_w_in, 16)
                sp.dma_start(wqx[:, :, J * ROPE:J * HD], d["W_qdec"].rearrange("p (g n) -> p g n", g=G)).then_inc(dec_w_in, 16)
                for r in range(2):
                    rows = slice(r * KVR, (r + 1) * KVR)
                    sp.dma_start(wkx[rows, :, 0:J * CON], d["W_kdec"].rearrange("p (g n) -> p g n", g=G)).then_inc(dec_w_in, 16)
                    sp.dma_start(wkx[rows, :, J * CON:], d["W_vdec"].rearrange("p (g n) -> p g n", g=G)).then_inc(dec_w_in, 16)
                sp.dma_start(k["cos"][:], d["cos"].rearrange("(t p) r -> p t r", p=P)).then_inc(tab_in, 16)
                sp.dma_start(k["sin"][:], d["sin"].rearrange("(t p) r -> p t r", p=P)).then_inc(tab_in, 16)
                sp.wait_ge(tab_in, 32)

            @block.gpsimd
            def _(pool):
                step = Chain(pool, pool_step)
                step.did(pool.memset(k["ident"][:], 0.0))
                step.did(pool.memset(mask1[:], 0.0))
                step.did(pool.memset(mask2[:], 0.0))
                step.did(pool.memset(lowrow[:], -1.0))
                step.settle()
                step.did(pool.affine_select(out=k["ident"][:], in_=k["ident"][:], compare_op=ALU.not_equal, fill=1.0,
                                            base=0, pattern=[[-1, P]], channel_multiplier=1))
                step.did(pool.affine_select(out=mask1[:], in_=mask1[:], compare_op=ALU.is_ge, fill=-BIG,
                                            base=0, pattern=[[-1, P]], channel_multiplier=1))
                step.did(pool.affine_select(out=mask2[:], in_=mask2[:], compare_op=ALU.is_ge, fill=-BIG,
                                            base=0, pattern=[[1, P]], channel_multiplier=-1))
                step.did(pool.memset(lowrow[0:KVR, :], 0.0))
                step.settle()
                pool.tensor_copy(k["ident_b"][:], k["ident"][:])
                pool.tensor_copy(k["mask_qk"][:], mask1[:])
                pool.tensor_copy(k["mask_kq"][:], mask2[:]).then_inc(const_ready, 1)
                for n in range(POOL_WEIGHTS, NW):
                    tiles = slice(4 * n, 4 * n + 4)
                    pool.wait_ge(x_in[n], 16)
                    pool.wait_ge(wt_ready, 1)
                    pool.tensor_tensor(k["h"][:, tiles, :], xin[:, tiles, :],
                                       wt[:, tiles].rearrange("p (t a) -> p t a", a=1).to_broadcast([P, 4, D]),
                                       ALU.mult).then_inc(h_weighted, 1)
                step.did(pool.memset(k["vst"][:], 0.0))
                step.settle()
                step.did(pool.memset(k["vst"][:, :, :, :, CON:CON + 1], 1.0))
                step.settle()

            def energies(pe, n):
                pe.wait_ge(hid_ready, n + 1)
                for i in range(4):
                    t = 4 * n + i
                    last = pe.matmul(ps[2][:, t:t + 1], hid[:, n % 2, i * P:(i + 1) * P], w2[:], start=True, stop=True)
                last.then_inc(en_ps, 1)

            @block.tensor
            def _(pe):
                pe.wait_ge(tok_w_in, 64)
                for n in range(NW):
                    pe.wait_ge(xT_in[n], 16)
                    if n >= 2:
                        pe.wait_ge(hid_ready, n - 1)
                    for c in range(DC):
                        last = pe.matmul(ps[n % 2][:], w1[:, c, :], xT[:, c, n * W:(n + 1) * W],
                                         start=(c == 0), stop=(c == DC - 1))
                    last.then_inc(hid_ps, 1)
                    if n >= 1:
                        energies(pe, n - 1)
                energies(pe, NW - 1)
                pe.wait_ge(const_ready, 1)
                pe.wait_ge(low_w_in, 48)
                for stage, n in PREPARE:
                    if stage == "turn":
                        pe.wait_ge(xn_ready, 4 * n + 4)
                        for c in range(DC):
                            m = n * DC + c
                            if m >= 2:
                                pe.wait_ge(xn_turned, m - 1)
                            for i in range(4):
                                last = pe.transpose(ps[4 + m % 2][:, i * P:(i + 1) * P],
                                                    xn[:, 4 * n + i, c * P:(c + 1) * P], k["ident"][:])
                            last.then_inc(turned, 1)
                    elif stage == "rank":
                        pe.wait_ge(xn_turned, DC * n + 2)
                        if n == 0:
                            pe.wait_ge(diff_ready, 1)
                        if n >= 2:
                            pe.wait_ge(kvn_read, n - 1)
                        for i in range(4):
                            tok = slice((4 * n + i) * P, (4 * n + i + 1) * P)
                            for c in range(DC):
                                last = pe.matmul(ps[2 + n % 2][:, i * KVR:(i + 1) * KVR], k["xn"][:, c, tok], wkv[:, c, :],
                                                 start=(c == 0), stop=(c == DC - 1))
                        last.then_inc(kv_ps, 1)
                        if n >= 2:
                            pe.wait_ge(qc_ready, n - 1)
                        for c in range(DC):
                            last = pe.matmul(ps[n % 2][:], wq[:, c, :], k["xn"][:, c, n * W:(n + 1) * W],
                                             start=(c == 0), stop=(c == DC - 1))
                        last.then_inc(qc_ps, 1)
                    elif stage == "stack":
                        pe.wait_ge(kvn_ready, n + 1)
                        if n >= 2:
                            pe.wait_ge(kv_split, n - 1)
                        for i in range(4):
                            last = pe.transpose(ps[6 + n % 2][:, i * P:(i + 1) * P], kvd[:, 4 * n + i], k["ident"][:])
                        last.then_inc(kv_turned, 1)

            @block.scalar
            def _(act):
                act.wait_ge(tok_w_in, 64)
                for n in range(NW):
                    act.wait_ge(hid_ps, n + 1)
                    if n >= 2:
                        act.wait_ge(en_ps, n - 1)
                    act.activation(hid[:, n % 2, :], ps[n % 2][:], ACT.Tanh, bias=b1[:, 0:1]).then_inc(hid_ready, 1)
                act.wait_ge(diff_ready, 1)
                act.activation(ex[:], de[:], ACT.Exp).then_inc(exp_ready, 1)
                for stage, n in PREPARE:
                    tiles = slice(4 * n, 4 * n + 4)
                    if stage == "norm":
                        act.wait_ge(var_ready, n + 1)
                        act.activation(sd[:, tiles], ve[:, tiles], ACT.Sqrt).then_inc(sd_ready, 1)
                    elif stage == "turn":
                        for c in range(DC):
                            m = n * DC + c
                            act.wait_ge(turned, m + 1)
                            act.activation(k["xn"][:, c, n * W:(n + 1) * W], ps[4 + m % 2][:], ACT.Copy).then_inc(xn_turned, 1)
                    elif stage == "rank":
                        act.wait_ge(kv_ps, n + 1)
                        act.activation(kvsq[:, tiles, :].rearrange("p t r -> p (t r)"), ps[2 + n % 2][:, 0:4 * KVR],
                                       ACT.Square).then_inc(kv_sq, 1)
                        act.wait_ge(qc_ps, n + 1)
                        act.activation(k["qc"][:, n * W:(n + 1) * W], ps[n % 2][:], ACT.Copy).then_inc(qc_ready, 1)
                    elif stage == "rms":
                        act.wait_ge(kv_mean, n + 1)
                        act.activation(kvs[:, tiles], kvm[:, tiles], ACT.Sqrt).then_inc(kv_sd, 1)
                    elif stage == "stack":
                        act.wait_ge(kv_turned, n + 1)
                        if n >= 2:
                            act.wait_ge(kv_split, n - 1)
                        act.activation(kvhi[:, n % 2, :], ps[6 + n % 2][:], ACT.Copy).then_inc(kv_hi, 1)

            @block.vector
            def _(dve):
                step = Chain(dve, dve_step)
                dve.memset(k["ones_rows"].bitcast(F32), 1.0)
                dve.memset(k["pmax"][:], LOWEST)
                dve.wait_ge(tok_w_in, 64)
                dve.wait_ge(en_ps, NW)
                step.did(dve.tensor_scalar(en[:], ps[2][:, 0:TT], b2[:, 0:1], None, ALU.add))
                step.settle()
                dve.tensor_tensor(de[:], en[:], en[:], ALU.subtract).then_inc(diff_ready, 1)
                dve.wait_ge(exp_ready, 1)
                step.did(dve.reciprocal(rs[:], ex[:]))
                step.settle()
                dve.tensor_tensor(wt[:], ex[:], rs[:], ALU.mult).then_inc(wt_ready, 1)
                dve.wait_ge(wt_ready, 1)
                dve.wait_ge(const_ready, 1)
                dve.wait_ge(low_w_in, 48)
                for stage, n in PREPARE:
                    tiles = slice(4 * n, 4 * n + 4)
                    if stage == "sums":
                        if n < POOL_WEIGHTS:
                            dve.wait_ge(x_in[n], 16)
                            for t in range(4 * n, 4 * n + 4):
                                step.did(dve.tensor_scalar(k["h"][:, t, :], xin[:, t, :], wt[:, t:t + 1], None, ALU.mult))
                            step.settle()
                        else:
                            dve.wait_ge(h_weighted, n - POOL_WEIGHTS + 1)
                        for t in range(4 * n, 4 * n + 4):
                            step.did(dve.bn_stats(stats[:, t, :], k["h"][:, t, :]))
                        step.settle()
                        for t in range(4 * n, 4 * n + 4):
                            step.did(dve.bn_aggr(mv[:, t, :], stats[:, t, :]))
                        step.settle()
                        dve.tensor_scalar(ve[:, tiles], mv[:, tiles, 1], 1e-5, None, ALU.add).then_inc(var_ready, 1)
                    elif stage == "norm":
                        dve.wait_ge(sd_ready, n + 1)
                        step.did(dve.reciprocal(rstd[:, tiles], sd[:, tiles]))
                        step.settle()
                        for t in range(4 * n, 4 * n + 4):
                            dve.tensor_scalar(xn[:, t, :], k["h"][:, t, :], mv[:, t, 0:1], rstd[:, t:t + 1],
                                              ALU.subtract, ALU.mult).then_inc(xn_ready, 1)
                    elif stage == "rank":
                        dve.wait_ge(kv_sq, n + 1)
                        step.did(dve.tensor_reduce(kvr[:, tiles], kvsq[:, tiles, :], AX.X, ALU.add))
                        step.settle()
                        dve.tensor_scalar(kvm[:, tiles], kvr[:, tiles], 1.0 / KVR, 1e-6, ALU.mult, ALU.add).then_inc(kv_mean, 1)
                    elif stage == "rms":
                        dve.wait_ge(kv_sd, n + 1)
                        step.did(dve.reciprocal(kvr[:, tiles], kvs[:, tiles]))
                        step.settle()
                        dve.tensor_tensor(
                            kvn[:, tiles, :], ps[2 + n % 2][:, 0:4 * KVR].rearrange("p (t r) -> p t r", r=KVR),
                            kvr[:, tiles].rearrange("p (t a) -> p t a", a=1).to_broadcast([P, 4, KVR]), ALU.mult).then_inc(kvn_read, 1)
                        dve.wait_ge(kvn_read, n + 1)
                        for r in range(2):
                            last = dve.tensor_tensor(kvd[:, tiles, r * KVR:(r + 1) * KVR], kvn[:, tiles, :],
                                                     gkv[:].rearrange("p (a r) -> p a r", a=1).to_broadcast([P, 4, KVR]), ALU.mult)
                        last.then_inc(kvn_ready, 1)
                    elif stage == "stack":
                        dve.wait_ge(kv_hi, n + 1)
                        dve.scalar_tensor_tensor(out=k["kv"][:, n * W:(n + 1) * W], in0=kvhi[:, n % 2, :].bitcast(F32),
                                                 scalar=lowrow[:, 0:1], in1=ps[6 + n % 2][:],
                                                 op0=ALU.mult, op1=ALU.add).then_inc(kv_split, 1)


def chunks():
    for t in range(BT):
        for ck in range(t // 4 + 1):
            yield t, ck, min(W, (t + 1) * P - ck * W)


def steps():
    for c in range(BT // 4):
        for kt in range(4 * c + 4):
            yield c, kt, max(0, kt - 4 * c) * P


CH = list(chunks())
ST = list(steps())
NC, NS = len(CH), len(ST)
EARLY = [x for x in range(NC) if CH[x][0] < 4]
LATE = [x for x in range(NC) if CH[x][0] >= 4]
RAWS = BT
TILES = ((0, 3), (3, 6), (6, 8), (8, 8))
VALUES = ((0, 3), (3, 5), (5, 9), (9, NS))
NV = len(VALUES)


def slot(tiles):
    first, after = tiles
    order = """S2 S3 V0 X0 S4 T1 X1 L1 X2 S5 P0 X3 S6 V1 S7 X4 X5 P1 S8 X6 X7 S9 X8 X9
               P2 S10 X10 X11 S11 V2 U0 M0 V3 K0 N0 N1 O0"""
    for event in order.split():
        what, i = event[0], int(event[1:])
        if what != "P":
            yield what, i
        elif first + i < after:
            yield what, first + i


def slots(g, last):
    for b in range(B):
        half = g * 2 + b
        final = last and b == B - 1
        for j in range(J):
            tiles = (0, 0) if final else TILES[j]
            left_out = "" if not final or j < J - 2 else "UK" if j == J - 2 else "UKNTLXM"
            yield half * J + j, half, j, b, [e for e in slot(tiles) if e[0] not in left_out]


def attention(nc, k):
    with ExitStack() as ctx:
        def sb(name, shape, dt=F32):
            return ctx.enter_context(nc.sbuf_tensor(name, shape, dt))

        def sem(name):
            return ctx.enter_context(nc.semaphore(name))

        Q0 = 2 * J * ROPE
        V0 = Q0 + 2 * J * CON
        SCALE = float(1.0 / (float(HD) ** 0.5))
        raw = sb("raw", [P, RAWS, 2 * J * ROPE])
        roc = sb("roc", [P, 2, 2 * J, ROPE])
        ros = sb("ros", [P, 2, 2 * J, ROPE])
        qk = sb("qk", [P, 2, BT, J, 2, LOW])
        mq = sb("mq", [P, 2, BT, J, CON + 2], F32R)
        prob = sb("prob", [P, NS, W])
        mx = sb("mx", [P, 2, BT])
        osb = sb("osb", [P, 2 * P])
        rcp = sb("rcp", [P, BT])
        nothing = sb("nothing", [HD, 1])
        kst, qa, qb = k["kst"], k["qa"], k["qb"]
        xn, qc, kv, vst, att = (k[n] for n in ("xn", "qc", "kv", "vst", "att"))
        ident, ident_b, mask_qk, mask_kq = (k[n] for n in ("ident", "ident_b", "mask_qk", "mask_kq"))

        prep = [ctx.enter_context(nc.psum_tensor(f"prep{i}", [P, W], F32)) for i in range(2)]
        mxp = [ctx.enter_context(nc.psum_tensor(f"mxp{i}", [P, W], F32)) for i in range(2)]
        sc = [ctx.enter_context(nc.psum_tensor(f"sc{i}", [P, W], F32)) for i in range(2)]
        acc = ctx.enter_context(nc.psum_tensor("acc", [P, W], F32))
        otr = ctx.enter_context(nc.psum_tensor("otr", [P, W], F32))

        (proj_done, raw_ready, arr_ready, qk_turned, khi_ready, klo_ready, qa_ready, qa2_ready, qb_ready, max_ps, max_taken,
         mcol_ready, m_turned, mrow_ready, mrow2_ready, score_ps, exp_done, av_done, o_taken, o_turned, att_ready,
         pool_step, dve_step, o_step, arr_step, first_arr, pads_ready, pad_step) = (sem(n) for n in (
             "proj_done", "raw_ready", "arr_ready", "qk_turned", "khi_ready", "klo_ready", "qa_ready", "qa2_ready", "qb_ready",
             "max_ps", "max_taken", "mcol_ready", "m_turned", "mrow_ready", "mrow2_ready", "score_ps", "exp_done", "av_done",
             "o_taken", "o_turned", "att_ready", "at_pool_step", "at_dve_step", "o_step", "arr_step", "first_arr", "pads_ready", "pad_step"))

        def next_half(g, b):
            return (g, 1) if b == 0 else (g + 1, 0)

        def bank(n, t):
            return prep[t % 2 if isinstance(n, int) and n == 0 else 0]

        def arrange(eng, step, before, n, b, t, done):
            u, w = t % 2, t % RAWS
            eng.wait_ge(raw_ready, n * BT + (t + 1))
            rope = raw[:, w, :].rearrange("p (h r) -> p h r", r=ROPE)
            cos = k["cos"][:, t:t + 1, :].to_broadcast([P, 2 * J, ROPE])
            eng.tensor_tensor(roc[:, u], rope, cos, ALU.mult)
            for lo, hi in ((0, ROPE // 2), (ROPE // 2, 0)):
                sin = k["sin"][:, t:t + 1, lo:lo + ROPE // 2].to_broadcast([P, 2 * J, ROPE // 2])
                last = eng.tensor_tensor(ros[:, u, :, lo:lo + ROPE // 2], rope[:, :, hi:hi + ROPE // 2], sin, ALU.mult)
            last.then_inc(step, 1)
            eng.wait_ge(step, before + 1)
            eng.tensor_tensor(qk[:, b, t, :, 1, 0:ROPE], roc[:, u, 0:J], ros[:, u, 0:J], ALU.add)
            eng.tensor_tensor(qk[:, b, t, :, 0, 0:ROPE], roc[:, u, J:2 * J], ros[:, u, J:2 * J],
                              ALU.add).then_inc(done, 1)

        with nc.Block() as block:
            @block.tensor
            def _(pe):
                def project(g, b, n, t):
                    if isinstance(n, int) and n == 0:
                        if t >= 2:
                            pe.wait_ge(raw_ready, t - 1)
                    else:
                        pe.wait_ge(raw_ready, n * BT + t)
                    out = bank(n, t)
                    tok = slice((b * BT + t) * P, (b * BT + t + 1) * P)
                    cols = bass.ds(g * J * ROPE, J * ROPE)
                    for c in range(DC):
                        pe.matmul(out[:, 0:J * ROPE], xn[:, c, tok], k["wkr"][:, c, cols], start=(c == 0), stop=(c == DC - 1))
                    pe.matmul(out[:, J * ROPE:J * (ROPE + HD)], qc[:, tok], k["wqx"][:, bass.ds(g, 1), :], start=True, stop=True)
                    pe.matmul(out[:, J * (ROPE + HD):7 * J * CON], kv[:, tok].bitcast(F32), k["wkx"][:, bass.ds(g, 1), :],
                              start=True, stop=True).then_inc(proj_done, 1)

                def turn(hd, j, b, hh):
                    pe.wait_ge(qb_ready, 1 + hd * 2 + hh)
                    for i in range(4):
                        last = pe.transpose(prep[1][0:ROWS, i * P:(i + 1) * P],
                                            qk[:, b, 4 * hh + i, j].rearrange("p s x -> p (s x)")[:, 0:ROWS], ident[:])
                    last.then_inc(qk_turned, 1)

                def maximum(hd, r, x):
                    t, ck, w = CH[x]
                    pe.wait_ge(klo_ready, 1 + hd * 2 + (1 + t // 4))
                    pe.wait_ge(qa2_ready, 1 + hd * 2 + (1 + t // 4))
                    pe.wait_ge(qb_ready, 1 + hd * 2 + (1 + t // 4))
                    if x < 2:
                        pe.wait_ge((mrow_ready, mrow2_ready)[x], 1 + hd)
                    else:
                        pe.wait_ge(max_taken, 1 + hd * NC + (x - 1))
                    out = mxp[x % 2]
                    q = slice(t * P, (t + 1) * P)
                    diagonal = ck == t // 4
                    full = max(w, FULL)
                    keys = kst[0:ROWS, r, ck * W:ck * W + full]
                    pe.matmul(out[:, 0:full], qa[0:ROWS, r, q], keys, start=True, stop=False)
                    last = pe.matmul(out[:, 0:full], qb[:, r, q], keys, start=False, stop=not diagonal)
                    if diagonal:
                        last = pe.matmul(out[:, w - P:w], ident_b[:], mask_qk[:], start=False, stop=True)
                    last.then_inc(max_ps, 1)

                def turn_maxima(hd, b, j):
                    pe.wait_ge(mcol_ready, hd + 1)
                    for hh in range(2):
                        for i in range(4):
                            last = pe.transpose(mxp[hh][0:CON + 2, i * P:(i + 1) * P],
                                                mq[:, b, 4 * hh + i, j, :].bitcast(F32), ident[:])
                        last.then_inc(m_turned, 1)

                def score(hd, r, u):
                    c, kt, lo = ST[u]
                    if kt == 0:
                        pe.wait_ge((mrow_ready, mrow2_ready)[c], 1 + hd + 1)
                    if not (isinstance(hd, int) and hd * NS + u < 2):
                        pe.wait_ge(exp_done, 1 + hd * NS + (u - 1))
                    left = min(lo, W - FULL)
                    q = slice(c * W + left, (c + 1) * W)
                    key = slice(kt * P, (kt + 1) * P)
                    out = sc[u % 2]
                    diagonal = kt >= 4 * c
                    pe.matmul(out[:, left:W], kst[:, r, key], qa[:, r, q], start=True, stop=False)
                    last = pe.matmul(out[:, left:W], kst[0:ROWS, r, key], qb[:, r, q], start=False, stop=not diagonal)
                    if diagonal:
                        last = pe.matmul(out[:, lo:lo + P], ident_b[:], mask_kq[:], start=False, stop=True)
                    last.then_inc(score_ps, 1)

                def values(hd, j, b, v):
                    if v == 0:
                        pe.wait_ge(o_taken, 1 + hd)
                    for u in range(*VALUES[v]):
                        c, kt, lo = ST[u]
                        pe.wait_ge(exp_done, 1 + hd * NS + (u + 1))
                        for i in range(lo // P, 4):
                            last = pe.matmul(acc[32 * i:32 * i + 32, c * P:(c + 1) * P], vst[:, b, kt, j, :],
                                             prob[:, u, i * P:(i + 1) * P], start=(kt == 0), stop=(kt == 4 * c + i))
                    last.then_inc(av_done, 1)

                def turn_output(hd):
                    pe.wait_ge(o_taken, 1 + hd + 1)
                    pe.wait_ge(att_ready, 1 + hd)
                    for c in range(2):
                        last = pe.transpose(otr[:, c * P:(c + 1) * P], osb[:, c * P:(c + 1) * P], ident[:])
                    last.then_inc(o_turned, 1)

                def group(g, last):
                    for hd, half, j, b, events in slots(g, last):
                        ng, nb = next_half(g, b)
                        nj, tb = (j + 1, b) if j < J - 1 else (0, nb)
                        for what, i in events:
                            if what == "S":
                                score(hd, j % 2, i)
                            elif what == "V":
                                values(hd, j, b, i)
                            elif what == "N":
                                score(hd + 1, nj % 2, i)
                            elif what == "T":
                                if j == J - 1:
                                    pe.wait_ge(arr_ready, 1 + half * BT + BT)
                                turn(hd + 1, nj, tb, i)
                            elif what == "U":
                                if j == J - 2:
                                    pe.wait_ge(arr_ready, 1 + half * BT + BT // 2)
                                turn(hd + 2, (j + 2) % J, b if j < J - 2 else nb, i)
                            elif what == "X":
                                maximum(hd + 1, nj % 2, i)
                            elif what == "M":
                                turn_maxima(hd + 1, tb, nj)
                            elif what == "P":
                                project(ng, nb, half + 1, i)
                            elif what == "O":
                                turn_output(hd)

                head_start(pe, qk_turned, av_done, o_turned)
                for t in range(BT):
                    project(0, 0, 0, t)
                for hh in range(2):
                    pe.wait_ge(first_arr, 4 * hh + 4)
                    if hh == 0:
                        pe.wait_ge(pads_ready, 2)
                        pe.wait_ge(raw_ready, BT)
                    turn(0, 0, 0, hh)
                    for x in EARLY if hh == 0 else LATE:
                        maximum(0, 0, x)
                turn(1, 1, 0, 0)
                turn_maxima(0, 0, 0)
                for u in range(2):
                    score(0, 0, u)
                with pe.Fori(0, G - 1) as g:
                    group(g, False)
                group(G - 1, True)

            @block.scalar
            def _(act):
                def take_raw(n, b, t):
                    act.wait_ge(proj_done, n * BT + (t + 1))
                    if not (isinstance(n, int) and n == 0):
                        act.wait_ge(qk_turned, 1 + n * (2 * J) - 2 * J + 2)
                        act.wait_ge(av_done, 1 + n * (NV * J) - NV * J)
                    src = bank(n, t)
                    content = src[:, Q0:V0].rearrange("p (s h r) -> p h s r", s=2, r=CON)
                    act.activation(raw[:, t % RAWS, :], src[:, 0:Q0], ACT.Copy)
                    act.activation(qk[:, b, t, :, :, ROPE:HD], content, ACT.Copy)
                    act.activation(mq[:, b, t, :, 0:CON], content[:, :, 0, :], ACT.Copy)
                    act.activation(vst[:, b, t, :, 0:CON], src[:, V0:V0 + J * CON].rearrange("p (h r) -> p h r", r=CON),
                                   ACT.Copy).then_inc(raw_ready, 1)

                def operands(hd, r, hh):
                    cols = slice(hh * W, (hh + 1) * W)
                    act.wait_ge(qk_turned, 1 + hd * 2 + (hh + 1))
                    act.activation(kst[LOW:ROWS, r, cols], prep[1][LOW:ROWS, :], ACT.Copy).then_inc(khi_ready, 1)
                    act.activation(qa[0:HD, r, cols], prep[1][0:HD, :], ACT.Copy).then_inc(qa_ready, 1)

                def max_rows(hd, r):
                    act.wait_ge(m_turned, hd * 2 + 1)
                    act.activation(qa[ROWS - CON:ROWS + 2, r, 0:W], mxp[0][0:CON + 2, :], ACT.Copy).then_inc(mrow_ready, 1)

                def exponential(hd, u):
                    lo = ST[u][2]
                    act.wait_ge(score_ps, hd * NS + (u + 1))
                    if u < 2 and not (isinstance(hd, int) and hd == 0):
                        act.wait_ge(av_done, 1 + hd * NV - NV + 1)
                    elif u >= 2:
                        act.wait_ge(av_done, 1 + hd * NV)
                    act.activation(prob[:, u, lo:W], sc[u % 2][:, lo:W], ACT.Exp, scale=SCALE).then_inc(exp_done, 1)

                def group(g, last):
                    for hd, half, j, b, events in slots(g, last):
                        for what, i in events:
                            if what == "S":
                                exponential(hd, i)
                            elif what == "N":
                                exponential(hd + 1, i)
                            elif what == "T":
                                operands(hd + 1, (j + 1) % 2, i)
                            elif what == "K":
                                operands(hd + 2, j % 2, i)
                            elif what == "M":
                                max_rows(hd + 1, (j + 1) % 2)
                            elif what == "P":
                                take_raw(half + 1, 1 - b, i)

                head_start(act, exp_done, mrow_ready)
                for t in range(BT):
                    take_raw(0, 0, t)
                act.wait_ge(pads_ready, 2)
                for hh in range(2):
                    operands(0, 0, hh)
                operands(1, 1, 0)
                max_rows(0, 0)
                for u in range(2):
                    exponential(0, u)
                with act.Fori(0, G - 1) as g:
                    group(g, False)
                group(G - 1, True)

            @block.gpsimd
            def _(pool):
                for i, pad in enumerate((kst[HD - CON:LOW], qa[HD - CON:LOW], qb[0:LOW])):
                    pool.memset(pad.bitcast(F32), 0.0).then_inc(pad_step, 1)
                    pool.wait_ge(pad_step, i + 1)
                pool.memset(qk[:].rearrange("p b t j s x -> p (b t j) (s x)")[:, :, HD:LOW], 0.0).then_inc(pads_ready, 1)
                def second_queries(hd, r, hh):
                    cols = slice(hh * W, (hh + 1) * W)
                    pool.wait_ge(qa_ready, hd * 2 + (hh + 1))
                    pool.wait_ge(qa2_ready, 1 + hd * 2 + hh)
                    pool.tensor_tensor(qa[LOW:ROWS, r, cols], qa[0:HD, r, cols].bitcast(F32),
                                       nothing[:].to_broadcast([HD, W]), ALU.add).then_inc(qa2_ready, 1)

                def group(g, last):
                    for hd, half, j, b, events in slots(g, last):
                        arranged = half * BT + (0 if last and b == B - 1 else TILES[j][0])
                        copied = hd * 2 + 3
                        for what, i in events:
                            if what == "P":
                                arranged = arranged + 1
                                pool.wait_ge(qa2_ready, 1 + copied)
                                arrange(pool, pool_step, half * BT + i, half + 1, 1 - b, i, arr_ready)
                            elif what == "T":
                                copied = copied + 1
                                pool.wait_ge(arr_ready, 1 + arranged)
                                second_queries(hd + 1, (j + 1) % 2, i)
                            elif what == "K":
                                copied = copied + 1
                                pool.wait_ge(arr_ready, 1 + arranged)
                                second_queries(hd + 2, j % 2, i)

                head_start(pool, arr_ready, qa2_ready)
                pool.wait_ge(pads_ready, 2)
                for hh in range(2):
                    second_queries(0, 0, hh)
                second_queries(1, 1, 0)
                pool.wait_ge(qa2_ready, 4)
                pool.wait_ge(first_arr, BT)
                with pool.Fori(0, G - 1) as g:
                    group(g, False)
                group(G - 1, True)

            @block.vector
            def _(dve):
                def low_parts(hd, r, hh):
                    cols = slice(hh * W, (hh + 1) * W)
                    dve.wait_ge(khi_ready, hd * 2 + (hh + 1))
                    dve.tensor_tensor(kst[0:HD, r, cols], prep[1][LOW:ROWS, :],
                                      kst[LOW:ROWS, r, cols].bitcast(F32), ALU.subtract).then_inc(klo_ready, 1)
                    dve.wait_ge(qa_ready, hd * 2 + (hh + 1))
                    dve.tensor_tensor(qb[LOW:ROWS, r, cols], prep[1][0:HD, :],
                                      qa[0:HD, r, cols].bitcast(F32), ALU.subtract).then_inc(qb_ready, 1)

                def maximum(hd, x):
                    t, ck, w = CH[x]
                    dve.wait_ge(max_ps, hd * NC + (x + 1))
                    dve.tensor_reduce(k["pmax"][:, ck, t:t + 1], mxp[x % 2][:, 0:w], AX.X, ALU.max).then_inc(max_taken, 1)

                def maxima(hd, r, b, j):
                    dve.wait_ge(max_taken, 1 + hd * NC + NC)
                    dve.tensor_tensor(mx[:, r], k["pmax"][:, 0, :], k["pmax"][:, 1, :], ALU.max).then_inc(dve_step, 1)
                    dve.wait_ge(dve_step, hd * 2 + 1)
                    dve.tensor_scalar(mq[:, b, :, j, CON], mx[:, r], -1.0, None, ALU.mult).then_inc(dve_step, 1)
                    dve.wait_ge(dve_step, hd * 2 + 2)
                    dve.scalar_tensor_tensor(out=mq[:, b, :, j, CON + 1], in0=mx[:, r], scalar=-1.0,
                                             in1=mq[:, b, :, j, CON].bitcast(F32), op0=ALU.mult, op1=ALU.subtract).then_inc(mcol_ready, 1)

                def max_rows(hd, r):
                    dve.wait_ge(m_turned, hd * 2 + 2)
                    dve.tensor_copy(qa[ROWS - CON:ROWS + 2, r, W:2 * W], mxp[1][0:CON + 2, :]).then_inc(mrow2_ready, 1)

                def take_output(hd):
                    dve.wait_ge(av_done, 1 + hd * NV + NV)
                    dve.wait_ge(o_turned, 1 + hd)
                    dve.tensor_copy(osb[:], acc[:, 0:2 * P]).then_inc(o_taken, 1)

                def divide(hd, g, j, b):
                    dve.wait_ge(o_turned, 1 + hd + 1)
                    o = otr[:, 0:BT * 32].rearrange("p (t r) -> p t r", t=BT)
                    dve.wait_ge(att_ready, 1 + hd)
                    dve.reciprocal(rcp[:], o[:, :, CON]).then_inc(o_step, 1)
                    dve.wait_ge(o_step, hd + 1)
                    dst = att[:, b * BT:(b + 1) * BT, bass.ds((g * J + j) * CON, CON)]
                    dve.tensor_tensor(dst, o[:, :, 0:CON],
                                      rcp[:].rearrange("p (t a) -> p t a", a=1).to_broadcast([P, BT, CON]),
                                      ALU.mult).then_inc(att_ready, 1)

                def group(g, last):
                    for hd, half, j, b, events in slots(g, last):
                        for what, i in events:
                            if what == "V" and i == NV - 1:
                                take_output(hd)
                            elif what == "O":
                                divide(hd, g, j, b)
                            elif what == "L":
                                low_parts(hd + 1, (j + 1) % 2, i)
                            elif what == "K":
                                low_parts(hd + 2, j % 2, i)
                            elif what == "X":
                                maximum(hd + 1, i)
                            elif what == "M":
                                maxima(hd + 1, (j + 1) % 2, b if j < J - 1 else 1 - b, (j + 1) % J)
                                max_rows(hd + 1, (j + 1) % 2)
                head_start(dve, klo_ready, qb_ready, max_taken, mrow2_ready, o_taken, att_ready)
                dve.memset(nothing[:], 0.0).then_inc(pads_ready, 1)
                for t in range(BT):
                    arrange(dve, arr_step, t, 0, 0, t, first_arr)
                for hh in range(2):
                    low_parts(0, 0, hh)
                    for x in EARLY if hh == 0 else LATE:
                        maximum(0, x)
                low_parts(1, 1, 0)
                maxima(0, 0, 0, 0)
                max_rows(0, 0)
                with dve.Fori(0, G - 1) as g:
                    group(g, False)
                group(G - 1, True)


def experts(nc, d, k):
    with ExitStack() as ctx:
        def sb(name, shape, dt=F32):
            return ctx.enter_context(nc.sbuf_tensor(name, shape, dt))

        def sem(name):
            return ctx.enter_context(nc.semaphore(name))

        att, h, ident = k["att"], k["h"], k["ident"]
        wo = sb("wo", [P, DC, D])
        attT = sb("attT", [P, DC, B * T])
        stats = sb("stats2", [P, TT, 6])
        mv = sb("mv2", [P, TT, 2])
        ve = sb("ve2", [P, TT])
        sd = sb("sd2", [P, TT])
        rstd = sb("rstd2", [P, TT])
        xn = att
        yT = attT
        yh = sb("yh", [P, DC, B * T], F32R)
        yl = sb("yl", [P, DC, B * T], F32R)
        gw = sb("gw", [P, DC, 32])
        lgs = sb("lgs", [P, W])
        gu = sb("gu", [P, 2, DC, 2 * F])
        dn = sb("dn", [P, 2, FC, D])
        guh = sb("guh", [P, 2, DC, 2 * F], F32R)
        gul = sb("gul", [P, 2, DC, 2 * F], F32R)
        dnh = sb("dnh", [P, 2, FC, D], F32R)
        dnl = sb("dnl", [P, 2, FC, D], F32R)
        sg = sb("sg", [P, 2, FC, W])
        hm = sb("hm", [P, 2, FC, W])
        hmh = sb("hmh", [P, 2, FC, W], F32R)
        hml = sb("hml", [P, 2, FC, W], F32R)
        R = {n: sb("r_" + n, [P, TT, E]) for n in ("lg", "ex", "p", "eq", "cd", "f1", "f2", "p2", "wd", "cb")}
        S = {n: sb("s_" + n, [P, TT]) for n in ("mx", "sum", "r", "m1", "m2", "c", "w1", "w2", "t")}
        rank = sb("rank", [P, E])
        M = {n: sb("m_" + n, [P, E, E]) for n in ("sim", "ms", "eq", "cd", "map", "id", "t")}
        V = {n: sb("v_" + n, [P, E]) for n in ("pres", "prim", "neg", "bs", "c", "go", "stay")}
        prod = sb("prod", [P, TT, E, E])
        ones = sb("ones", [P, P])
        iot = sb("iot", [P, E])

        ps = [ctx.enter_context(nc.psum_tensor(f"pc{i}", [P, W], F32)) for i in range(8)]

        def quarter(i, r=0):
            return ps[4 + 2 * r + i // 2][:, (i % 2) * D:(i % 2 + 1) * D]

        (wo_in, gw_in, at_turned, at_ready, o_ps, h_ready, var_ready, sd_ready, xn_ready, y_turned, y_hi, y_lo,
         lg_ps, lg_max, ex_ready, pres_ready, pres_ps, cb_ready, w_split, gu_ps, sg_ready, hm_ready,
         hmh_ready, hml_ready, w_hi, dn_ps, acc_done, dve_step, pool_step, out_done, const2, gw_zero, gw_ready, lg_raw, lg_taken, prim_ready) = (sem(n) for n in (
             "wo_in", "gw_in", "at_turned", "at_ready", "o_ps", "h_ready", "var2_ready", "sd2_ready", "xn2_ready",
             "y_turned", "y_hi", "y_lo", "lg_ps", "lg_max", "ex2_ready", "pres_ready", "pres_ps", "cb_ready",
             "w_split", "gu_ps", "sg_ready", "hm_ready", "hmh_ready", "hml_ready", "w_hi", "dn_ps",
             "acc_done", "dve2_step", "pool2_step", "out_done", "const2",
             "gw_zero", "gw_ready", "lg_raw", "lg_taken", "prim_ready"))

        ex_in = [sem(f"ex_in{u}") for u in range(2)]

        with nc.Block() as block:
            @block.sync
            def _(sp):
                sp.dma_start(wo[:], d["W_o"].rearrange("(c p) n -> p c n", p=P)).then_inc(wo_in, 16)
                sp.wait_ge(gw_zero, 1)
                sp.dma_start(gw[:, :, 0:E], d["gateT"].rearrange("(c p) e -> p c e", p=P)).then_inc(gw_ready, 16)
                sp.dma_start(M["sim"][:].rearrange("p a b -> p (a b)"),
                             d["sim"].rearrange("a b -> (a b)").rearrange("(o n) -> o n", o=1).to_broadcast([P, E * E])).then_inc(gw_in, 16)
                with sp.Fori(0, E // 2) as e2:
                    for u in range(2):
                        e = e2 * 2 + u
                        sp.wait_ge(w_split, 1 + e2 * 2)
                        sp.dma_start(gu[:, u], d["guT"][bass.ds(e, 1)].rearrange("o (c p) f -> p (o c) f", p=P)).then_inc(ex_in[u], 16)
                        sp.dma_start(dn[:, u], d["dnT"][bass.ds(e, 1)].rearrange("o (c p) f -> p (o c) f", p=P)).then_inc(ex_in[u], 16)
                for n in range(NW):
                    tiles = slice(4 * n, 4 * n + 4)
                    sp.wait_ge(acc_done, 1 + (E - 1) * NW + (n + 1))
                    sp.dma_start(d["out"].rearrange("(t p) e -> p t e", p=P)[:, tiles, :], h[:, tiles, :]).then_inc(out_done, 16)
                sp.wait_ge(out_done, 16 * NW)

            @block.gpsimd
            def _(pool):
                pool.memset(gw[:], 0.0).then_inc(gw_zero, 1)
                pool.iota(iot[:], pattern=[[-1, E]], base=E, channel_multiplier=0,
                          allow_small_or_imprecise_dtypes=True).then_inc(pool_step, 1)
                pool.memset(M["id"][:], 0.0).then_inc(pool_step, 1)
                pool.wait_ge(pool_step, 2)
                pool.affine_select(out=M["id"][:], in_=M["id"][:], compare_op=ALU.not_equal, fill=1.0,
                                   base=0, pattern=[[1, E], [-1, E]], channel_multiplier=0).then_inc(const2, 1)
                pool.memset(ones[:], 1.0).then_inc(const2, 1)
                head_start(pool, w_split)

                def low_weights(e, u):
                    pool.wait_ge(w_hi, e + 1)
                    pool.tensor_tensor(gul[:, u], gu[:, u], guh[:, u].bitcast(F32), ALU.subtract)
                    pool.tensor_tensor(dnl[:, u], dn[:, u], dnh[:, u].bitcast(F32), ALU.subtract).then_inc(w_split, 1)

                low_weights(0, 0)
                for n in range(NW):
                    for c in range(DC):
                        cols = slice(n * W, (n + 1) * W)
                        pool.wait_ge(y_hi, n * DC + (c + 1))
                        pool.tensor_tensor(yl[:, c, cols], yT[:, c, cols], yh[:, c, cols].bitcast(F32), ALU.subtract).then_inc(y_lo, 1)
                low_weights(1, 1)
                with pool.Fori(1, E // 2) as e2:
                    for u in range(2):
                        low_weights(e2 * 2 + u, u)

            @block.tensor
            def _(pe):
                for n in range(NW):
                    for c in range(DC):
                        m = n * DC + c
                        if m >= 4:
                            pe.wait_ge(at_ready, m - 3)
                        for i in range(4):
                            last = pe.transpose(ps[m % 4][:, i * P:(i + 1) * P], att[:, 4 * n + i, c * P:(c + 1) * P], ident[:])
                        last.then_inc(at_turned, 1)
                pe.wait_ge(wo_in, 16)

                def residual(n):
                    pe.wait_ge(at_ready, (n + 1) * DC)
                    for t in range(4 * n, 4 * n + 4):
                        if t >= 4 and t % 2 == 0:
                            pe.wait_ge(h_ready, t - 2)
                        for c in range(DC):
                            last = pe.matmul(quarter(t % 4), attT[:, c, t * P:(t + 1) * P], wo[:, c, :], start=(c == 0), stop=(c == DC - 1))
                        last.then_inc(o_ps, 1)

                def turn(n):
                    pe.wait_ge(xn_ready, 4 * n + 4)
                    for c in range(DC):
                        m = n * DC + c
                        if m >= 2:
                            pe.wait_ge(y_hi, m - 1)
                        for i in range(4):
                            last = pe.transpose(ps[6 + m % 2][:, i * P:(i + 1) * P], xn[:, 4 * n + i, c * P:(c + 1) * P], ident[:])
                        last.then_inc(y_turned, 1)

                def logits():
                    pe.wait_ge(gw_ready, 16)
                    pe.wait_ge(y_hi, NW * DC)
                    for c in range(DC):
                        for n in range(NW):
                            last = pe.matmul(ps[6][32 * n:32 * n + 32, :], gw[:, c, :], yT[:, c, n * W:(n + 1) * W],
                                             start=(c == 0), stop=(c == DC - 1))
                    last.then_inc(lg_raw, 1)

                def turn_logits():
                    pe.wait_ge(lg_taken, 1)
                    for i in range(4):
                        last = pe.transpose(ps[7][:, i * P:(i + 1) * P], lgs[:, i * P:(i + 1) * P], ident[:])
                    last.then_inc(lg_ps, 1)

                def presence():
                    pe.wait_ge(pres_ready, 1)
                    pe.wait_ge(const2, 2)
                    pe.matmul(ps[6][:, 0:E], ones[:], V["pres"][:], start=True, stop=True).then_inc(pres_ps, 1)

                def up(e, u, n):
                    it = e * NW + n
                    cols = slice(n * W, (n + 1) * W)
                    if n == 0:
                        pe.wait_ge(w_split, 1 + e + 1)
                    if isinstance(e, int) and e == 0:
                        pe.wait_ge(y_lo, DC * (n + 1))
                    pe.wait_ge(hm_ready, 1 + it * FC)
                    for fc in range(FC):
                        for s in range(2):
                            f = slice(s * F + fc * P, s * F + (fc + 1) * P)
                            for c in range(DC):
                                last = three(pe, ps[2 * fc + s][:], (guh[:, u, c, f], gul[:, u, c, f]),
                                             (yh[:, c, cols], yl[:, c, cols]), c == 0, c == DC - 1)
                        last.then_inc(gu_ps, 1)

                def down(e, u, n):
                    it = e * NW + n
                    r = n % 2
                    pe.wait_ge(hml_ready, it * FC + FC)
                    if not (isinstance(it, int) and it == 0):
                        pe.wait_ge(acc_done, it)
                    for i in range(4):
                        tok = slice(i * P, (i + 1) * P)
                        for fc in range(FC):
                            last = three(pe, quarter(i, r), (hmh[:, r, fc, tok], hml[:, r, fc, tok]),
                                         (dnh[:, u, fc, :], dnl[:, u, fc, :]), fc == 0, fc == FC - 1)
                        last.then_inc(dn_ps, 1)

                def pair(e2, first):
                    for u in range(2):
                        for n in range(NW):
                            e = e2 * 2 + u
                            up(e, u, n)
                            if first and u == 0 and n == 0:
                                turn(2)
                                turn(3)
                                logits()
                                turn_logits()
                            elif first and u == 0 and n == 1:
                                presence()
                            elif first and u == 0 and n == 2:
                                pe.wait_ge(prim_ready, 1)
                            if n:
                                down(e, u, n - 1)
                            elif not (first and u == 0):
                                down(e - 1, 1 - u, NW - 1)

                for n in range(3):
                    residual(n)
                turn(0)
                residual(3)
                turn(1)
                pair(0, True)
                with pe.Fori(1, E // 2) as e2:
                    pair(e2, False)
                down(E - 1, 1, NW - 1)

            @block.scalar
            def _(act):
                def high_weights(e2, u, first):
                    act.wait_ge(ex_in[u], e2 * 32 + 32)
                    if not first:
                        act.wait_ge(dn_ps, e2 * (8 * NW) + (u - 1) * (4 * NW))
                        act.wait_ge(w_split, 1 + e2 * 2 + (u - 1))
                    act.activation(guh[:, u], gu[:, u], ACT.Copy)
                    act.activation(dnh[:, u], dn[:, u], ACT.Copy).then_inc(w_hi, 1)

                for n in range(NW):
                    for c in range(DC):
                        m = n * DC + c
                        act.wait_ge(at_turned, m + 1)
                        act.activation(attT[:, c, n * W:(n + 1) * W], ps[m % 4][:], ACT.Copy).then_inc(at_ready, 1)
                def deviation(n):
                    act.wait_ge(var_ready, n + 1)
                    act.activation(sd[:, 4 * n:4 * n + 4], ve[:, 4 * n:4 * n + 4], ACT.Sqrt).then_inc(sd_ready, 1)

                def high_tokens(n):
                    act.wait_ge(o_ps, 4 * n + 4)
                    for c in range(DC):
                        m = n * DC + c
                        cols = slice(n * W, (n + 1) * W)
                        act.wait_ge(y_turned, m + 1)
                        act.activation(yT[:, c, cols], ps[6 + m % 2][:], ACT.Copy)
                        act.activation(yh[:, c, cols], ps[6 + m % 2][:], ACT.Copy).then_inc(y_hi, 1)

                def silus(it, r):
                    for fc in range(FC):
                        act.wait_ge(gu_ps, it * FC + (fc + 1))
                        act.activation(sg[:, r, fc, :], ps[2 * fc][:], ACT.Silu).then_inc(sg_ready, 1)

                def high_hidden(it, r):
                    for fc in range(FC):
                        act.wait_ge(hm_ready, 1 + it * FC + (fc + 1))
                        act.activation(hmh[:, r, fc, :], hm[:, r, fc, :], ACT.Copy).then_inc(hmh_ready, 1)

                def pair(e2, first, more):
                    for u in range(2):
                        for n in range(NW):
                            it = e2 * (2 * NW) + (u * NW + n)
                            silus(it, n % 2)
                            if first and u == 0 and n == 0:
                                high_tokens(2)
                                high_tokens(3)
                            high_hidden(it, n % 2)
                            if first and u == 0 and n == 0:
                                act.wait_ge(lg_raw, 1)
                                act.activation(lgs[:], ps[6][:], ACT.Copy).then_inc(lg_taken, 1)
                                act.wait_ge(lg_max, 1)
                                act.activation(R["ex"][:], R["lg"][:], ACT.Exp).then_inc(ex_ready, 1)
                            if n == 2 and u == 0:
                                high_weights(e2, 1, first)
                            if n == 2 and u == 1 and more:
                                high_weights(e2 + 1, 0, False)

                high_weights(0, 0, True)
                deviation(0)
                deviation(1)
                high_tokens(0)
                deviation(2)
                high_tokens(1)
                deviation(3)
                pair(0, True, True)
                with act.Fori(1, E // 2 - 1) as e2:
                    pair(e2, False, True)
                pair(E // 2 - 1, False, False)

            @block.vector
            def _(dve):
                step = Chain(dve, dve_step)

                def did(ins):
                    step.did(ins)
                    step.settle()

                def add_attention(n):
                    for t in range(4 * n, 4 * n + 4):
                        dve.wait_ge(o_ps, t + 2 - t % 2)
                        dve.tensor_tensor(h[:, t, :], h[:, t, :], quarter(t % 4), ALU.add).then_inc(h_ready, 1)

                head_start(dve, hm_ready, acc_done)
                add_attention(0)
                for n in range(NW):
                    tiles = range(4 * n, 4 * n + 4)
                    dve.wait_ge(h_ready, 4 * n + 4)
                    for t in tiles:
                        step.did(dve.bn_stats(stats[:, t, :], h[:, t, :]))
                    step.settle()
                    for t in tiles:
                        step.did(dve.bn_aggr(mv[:, t, :], stats[:, t, :]))
                    step.settle()
                    dve.tensor_scalar(ve[:, 4 * n:4 * n + 4], mv[:, 4 * n:4 * n + 4, 1], 1e-5, None, ALU.add).then_inc(var_ready, 1)
                    if n + 1 < NW:
                        add_attention(n + 1)
                    dve.wait_ge(sd_ready, n + 1)
                    did(dve.reciprocal(rstd[:, 4 * n:4 * n + 4], sd[:, 4 * n:4 * n + 4]))
                    if n == 0:
                        dve.wait_ge(at_turned, NW * DC)
                    for t in tiles:
                        dve.tensor_scalar(xn[:, t, :], h[:, t, :], mv[:, t, 0:1], rstd[:, t:t + 1],
                                          ALU.subtract, ALU.mult).then_inc(xn_ready, 1)

                def gated(it, r):
                    for fc in range(FC):
                        dve.wait_ge(sg_ready, it * FC + (fc + 1))
                        dve.tensor_tensor(hm[:, r, fc, :], sg[:, r, fc, :], ps[2 * fc + 1][:], ALU.mult).then_inc(hm_ready, 1)
                    for fc in range(FC):
                        dve.wait_ge(hmh_ready, it * FC + (fc + 1))
                        dve.tensor_tensor(hml[:, r, fc, :], hm[:, r, fc, :], hmh[:, r, fc, :].bitcast(F32), ALU.subtract).then_inc(hml_ready, 1)

                def add_down(it, e, n):
                    for i in range(4):
                        t = 4 * n + i
                        dve.wait_ge(dn_ps, it * 4 + (i + 2 - i % 2))
                        last = dve.scalar_tensor_tensor(out=h[:, t, :], in0=quarter(i, n % 2),
                                                        scalar=R["cb"][:, t, bass.ds(e, 1)], in1=h[:, t, :],
                                                        op0=ALU.mult, op1=ALU.add)
                    last.then_inc(acc_done, 1)

                gated(0, 0)

                def wide(s):
                    return S[s][:].rearrange("p (t a) -> p t a", a=1).to_broadcast([P, TT, E])

                def each(v):
                    return v[:].rearrange("p (a e) -> p a e", a=1).to_broadcast([P, TT, E])

                dve.wait_ge(lg_ps, 1)
                lg = ps[7][:].rearrange("p (i n e) -> p n i e", n=NW, e=32)[:, :, :, 0:E]

                def by_bank(v):
                    return v.rearrange("p (n i) e -> p n i e", n=NW)

                did(dve.tensor_copy(by_bank(R["p2"][:]), lg))
                did(dve.tensor_reduce(S["mx"][:], R["p2"][:], AX.X, ALU.max))
                dve.tensor_tensor(R["lg"][:], R["p2"][:], wide("mx"), ALU.subtract).then_inc(lg_max, 1)
                dve.wait_ge(ex_ready, 1)
                did(dve.tensor_reduce(S["sum"][:], R["ex"][:], AX.X, ALU.add))
                did(dve.reciprocal(S["r"][:], S["sum"][:]))
                did(dve.tensor_tensor(R["p"][:], R["ex"][:], wide("r"), ALU.mult))
                dve.wait_ge(const2, 2)

                def largest(src, m, f):
                    did(dve.tensor_reduce(S[m][:], R[src][:], AX.X, ALU.max))
                    did(dve.tensor_tensor(R["eq"][:], R[src][:], wide(m), ALU.is_equal))
                    did(dve.tensor_tensor(R["cd"][:], R["eq"][:], each(iot), ALU.mult))
                    did(dve.tensor_reduce(S["c"][:], R["cd"][:], AX.X, ALU.max))
                    did(dve.tensor_tensor(R[f][:], each(iot), wide("c"), ALU.is_equal))

                largest("p", "m1", "f1")
                did(dve.scalar_tensor_tensor(out=R["p2"][:], in0=R["f1"][:], scalar=-2.0, in1=R["p"][:], op0=ALU.mult, op1=ALU.add))
                dve.tensor_reduce(V["pres"][:], R["f1"][:].rearrange("p t e -> p e t"), AX.X, ALU.add).then_inc(pres_ready, 1)
                gated(1, 1)
                dve.wait_ge(pres_ps, 1)
                dve.tensor_scalar(V["prim"][:], ps[6][:, 0:E], 0.5, None, ALU.is_ge).then_inc(prim_ready, 1)
                largest("p2", "m2", "f2")
                did(dve.tensor_tensor(S["t"][:], S["m1"][:], S["m2"][:], ALU.add))
                did(dve.tensor_scalar(S["t"][:], S["t"][:], 1e-12, None, ALU.max))
                did(dve.reciprocal(S["r"][:], S["t"][:]))
                did(dve.tensor_tensor(S["w1"][:], S["m1"][:], S["r"][:], ALU.mult))
                did(dve.tensor_tensor(S["w2"][:], S["m2"][:], S["r"][:], ALU.mult))
                did(dve.tensor_tensor(R["wd"][:], R["f1"][:], wide("w1"), ALU.mult))
                did(dve.tensor_tensor(R["cd"][:], R["f2"][:], wide("w2"), ALU.mult))
                did(dve.tensor_tensor(R["wd"][:], R["wd"][:], R["cd"][:], ALU.add))
                dve.wait_ge(dn_ps, 4)
                gated(2, 0)
                def over_i(v):
                    return v[:].rearrange("p (a e) -> p a e", a=1).to_broadcast([P, E, E])

                def over_j(v):
                    return v[:].rearrange("p (e a) -> p e a", a=1).to_broadcast([P, E, E])

                dve.wait_ge(gw_in, 16)
                dve.wait_ge(prim_ready, 1)
                did(dve.tensor_scalar(V["neg"][:], V["prim"][:], -LOWEST, LOWEST, ALU.mult, ALU.add))
                did(dve.tensor_tensor(M["ms"][:], M["sim"][:], over_i(V["prim"]), ALU.mult))
                did(dve.tensor_tensor(M["ms"][:], M["ms"][:], over_i(V["neg"]), ALU.add))
                did(dve.tensor_reduce(V["bs"][:], M["ms"][:], AX.X, ALU.max))
                did(dve.tensor_tensor(M["eq"][:], M["ms"][:], over_j(V["bs"]), ALU.is_equal))
                did(dve.tensor_tensor(M["cd"][:], M["eq"][:], over_i(iot), ALU.mult))
                did(dve.tensor_reduce(V["c"][:], M["cd"][:], AX.X, ALU.max))
                did(dve.tensor_tensor(M["map"][:], over_i(iot), over_j(V["c"]), ALU.is_equal))
                did(dve.tensor_scalar(V["go"][:], V["bs"][:], 0.7, None, ALU.is_ge))
                did(dve.tensor_tensor(V["go"][:], V["go"][:], V["prim"][:], ALU.is_gt))
                did(dve.tensor_scalar(V["stay"][:], V["go"][:], -1.0, 1.0, ALU.mult, ALU.add))
                did(dve.tensor_tensor(M["map"][:], M["map"][:], over_j(V["go"]), ALU.mult))
                did(dve.tensor_tensor(M["t"][:], M["id"][:], over_j(V["stay"]), ALU.mult))
                did(dve.tensor_tensor(M["map"][:], M["map"][:], M["t"][:], ALU.add))
                for j in range(E):
                    step.did(dve.tensor_tensor(prod[:, :, j, :], R["wd"][:], M["map"][:, :, j].rearrange("p (a e) -> p a e", a=1).to_broadcast([P, TT, E]), ALU.mult))
                step.settle()
                dve.tensor_reduce(R["cb"][:], prod[:], AX.X, ALU.add).then_inc(cb_ready, 1)
                dve.wait_ge(cb_ready, 1)

                def pair(e2, first):
                    for u in range(2):
                        for n in range(NW):
                            it = e2 * (2 * NW) + (u * NW + n)
                            if first and u == 0 and n < 3:
                                if n:
                                    add_down(n - 1, 0, n - 1)
                                continue
                            gated(it, n % 2)
                            if n:
                                add_down(it - 1, e2 * 2 + u, n - 1)
                            else:
                                add_down(it - 1, e2 * 2 + (u - 1), NW - 1)

                pair(0, True)
                with dve.Fori(1, E // 2) as e2:
                    pair(e2, False)
                add_down(E * NW - 1, E - 1, NW - 1)


def tower(nc, d):
    with ExitStack() as ctx:
        def sb(name, shape, dt=F32):
            return ctx.enter_context(nc.sbuf_tensor(name, shape, dt))

        k = {
            "h": sb("h", [P, TT, D]),
            "cos": sb("cos", [P, BT, ROPE]), "sin": sb("sin", [P, BT, ROPE]),
            "ident": sb("ident", [P, P]), "ident_b": sb("ident_b", [P, P], BF16),
            "mask_qk": sb("mask_qk", [P, P], BF16), "mask_kq": sb("mask_kq", [P, P], BF16),
            "pmax": sb("pmax", [P, 2, BT]),
        }
        with ExitStack() as inner:
            def sbi(name, shape, dt=F32):
                return inner.enter_context(nc.sbuf_tensor(name, shape, dt))

            att = sb("att", [P, TT, D])
            k.update({
                "xn": sbi("xnT", [P, DC, B * T]), "qc": sbi("qc", [P, B * T]), "kv": sbi("kv", [P, B * T], F32R),
                "wkr": sbi("wkr", [P, DC, HEADS * ROPE]), "wqx": sbi("wqx", [P, G, J * HD]),
                "wkx": sbi("wkx", [P, G, 2 * J * CON]),
                "vst": sbi("vst", [P, 2, BT, J, 32]),
                "kst": sbi("kst", [ROWS + 2, 2, T], F32R),
                "att": att,
            })
            k["ones_rows"] = k["kst"][ROWS - CON:ROWS + 2, :, :]
            prepare(nc, d, k)
            k["qa"] = sbi("qa", [ROWS + 2, 2, T], F32R)
            k["qb"] = sbi("qb", [ROWS, 2, T], F32R)
            attention(nc, k)
        experts(nc, d, k)


_WEIGHTS = ['L0_tok_W1', 'L0_tok_b1', 'L0_tok_W2', 'L0_tok_b2', 'L0_attn_W_kv', 'L0_attn_g_kv', 'L0_attn_W_kdec',
            'L0_attn_W_vdec', 'L0_attn_W_q', 'L0_attn_W_qdec', 'L0_attn_W_krope', 'L0_attn_W_qrope', 'L0_attn_W_o']


def kernel(**inputs):
    import numpy as np
    import concourse.bacc as bacc
    from concourse.bass_utils import run_bass_kernel_spmd

    nc = bacc.Bacc("TRN2", target_bir_lowering=False, num_devices=1, dynamic_dma_scratch_size=1024)
    nc.disable_value_cache = True
    x = np.asarray(inputs["x"])
    tokens = x.reshape(B * T, D)
    arrays = {n.split("_", 2)[2]: np.ascontiguousarray(inputs[n]) for n in _WEIGHTS}
    arrays["x"] = np.ascontiguousarray(tokens)
    arrays["xT"] = np.ascontiguousarray(tokens.T)
    arrays["gateT"] = np.ascontiguousarray(np.asarray(inputs["L0_ffn_gate_weight"]).T)
    arrays["guT"] = np.ascontiguousarray(np.asarray(inputs["L0_ffn_gate_up_proj"]).transpose(0, 2, 1))
    arrays["dnT"] = np.ascontiguousarray(np.asarray(inputs["L0_ffn_down_proj"]).transpose(0, 2, 1))
    arrays["sim"] = np.ascontiguousarray(inputs["L0_ffn_similarity_matrix"])
    inv_freq = 1.0 / 10000.0 ** (np.arange(0, ROPE, 2, dtype=np.float32) / ROPE)
    freqs = np.outer(np.arange(T, dtype=np.float32), inv_freq)
    arrays["cos"] = np.cos(np.concatenate([freqs, freqs], -1)).astype(np.float32)
    arrays["sin"] = np.sin(np.concatenate([-freqs, freqs], -1)).astype(np.float32)

    d = {n: nc.dram_tensor("in_" + n, a.shape, mybir.dt.from_np(a.dtype), kind="ExternalInput").ap()
         for n, a in arrays.items()}
    d["out"] = nc.dram_tensor("out_h", (B * T, D), F32, kind="ExternalOutput").ap()
    tower(nc, d)
    r = run_bass_kernel_spmd(nc, [{"in_" + n: a for n, a in arrays.items()}], core_ids=[0])
    return r.results[0]["out_h"].reshape(B, T, D)
```
